# Optimizing a Trainium2 kernel written in Bass

```python
import numpy as np
import jax
import jax.numpy as jnp

def _softmax(x, axis=-1):
    return jax.nn.softmax(x, axis=axis)

def _gelu(x):
    return jax.nn.gelu(x, approximate=True)

def _silu(x):
    return jax.nn.silu(x)

def _sigmoid(x):
    return jax.nn.sigmoid(x)

def _layernorm(x, axis=-1, eps=1e-05):
    m = jnp.mean(x, axis=axis, keepdims=True)
    v = jnp.var(x, axis=axis, keepdims=True)
    return (x - m) / jnp.sqrt(v + eps)

def _scatter_add(tgt, idx, src, axis=0):
    return tgt.at[idx].add(src)

def _segment_sum(src, seg, n):
    return jax.ops.segment_sum(src, seg, n)
kernel_name = 'mk_seq_preln_d1_jaxref_r4_847eed'

def setup_inputs(seed: int=0):
    np.random.seed(seed)
    _w = jnp.asarray

    def _L0_attn_setup():
        import jax, jax.numpy as jnp
        import numpy as np
        D_MODEL = 512
        N_HEADS = 8
        EXPAND_K = 1
        EXPAND_V = 2
        DK = D_MODEL * EXPAND_K // N_HEADS
        DV = D_MODEL * EXPAND_V // N_HEADS
        INTER = 1408
        EPS = 1e-06
        CHUNK = 64

        def rmsnorm(x, w, eps=EPS):
            return x * jax.lax.rsqrt(jnp.mean(x * x, axis=-1, keepdims=True) + eps) * w

        def rope(x):
            T, D = (x.shape[1], x.shape[-1])
            inv_freq = 1.0 / 10000.0 ** (jnp.arange(0, D, 2, dtype=jnp.float32) / D)
            ang = jnp.arange(T, dtype=jnp.float32)[:, None] * inv_freq
            cos = jnp.cos(ang)[None, :, None, :]
            sin = jnp.sin(ang)[None, :, None, :]
            x1, x2 = jnp.split(x, 2, axis=-1)
            return jnp.concatenate([x1 * cos - x2 * sin, x2 * cos + x1 * sin], axis=-1)

        def chunk_retention(q, k, v):
            B, T, H, Dk = q.shape
            Dv = v.shape[-1]
            C = CHUNK
            N = T // C
            gamma = 1.0 - jnp.exp2(-5.0 - jnp.arange(H, dtype=jnp.float32))
            i = jnp.arange(C, dtype=jnp.float32)
            diff = i[:, None] - i[None, :]
            Dmask = jnp.where(diff >= 0, gamma[:, None, None] ** diff, 0.0)
            cross_decay = gamma[:, None] ** (i[None, :] + 1.0)
            k_decay = gamma[:, None] ** (C - 1.0 - i[None, :])
            chunk_decay = gamma ** C
            to_chunks = lambda x: jnp.moveaxis(x.reshape(B, N, C, H, x.shape[-1]).transpose(0, 1, 3, 2, 4), 1, 0)
            qc, kc, vc = (to_chunks(q), to_chunks(k), to_chunks(v))

            def body(S, inp):
                qb, kb, vb = inp
                attn = jnp.einsum('bhid,bhjd->bhij', qb, kb) * Dmask
                o_intra = jnp.einsum('bhij,bhje->bhie', attn, vb)
                o_cross = jnp.einsum('bhid,bhde->bhie', qb * cross_decay[None, :, :, None], S)
                S = chunk_decay[None, :, None, None] * S + jnp.einsum('bhid,bhie->bhde', kb * k_decay[None, :, :, None], vb)
                return (S, o_intra + o_cross)
            S0 = jnp.zeros((B, H, Dk, Dv), q.dtype)
            _, o = jax.lax.scan(body, S0, (qc, kc, vc))
            return jnp.moveaxis(o, 0, 1).transpose(0, 1, 3, 2, 4).reshape(B, T, H, Dv)
        key = jax.random.key(seed)
        ks = jax.random.split(key, 12)
        d = D_MODEL
        s = lambda fan_in: 1.0 / np.sqrt(fan_in)
        return {'hidden_states': jax.random.normal(ks[0], (2, 512, d), jnp.float32), 'attn_norm_w': jnp.ones((d,), jnp.float32), 'q_w': jax.random.normal(ks[1], (d, d * EXPAND_K), jnp.float32) * s(d), 'k_w': jax.random.normal(ks[2], (d, d * EXPAND_K), jnp.float32) * s(d), 'v_w': jax.random.normal(ks[3], (d, d * EXPAND_V), jnp.float32) * s(d), 'g_w': jax.random.normal(ks[4], (d, d * EXPAND_V), jnp.float32) * s(d), 'o_w': jax.random.normal(ks[5], (d * EXPAND_V, d), jnp.float32) * s(d * EXPAND_V), 'gnorm_w': jnp.ones((DV,), jnp.float32), 'mlp_norm_w': jnp.ones((d,), jnp.float32), 'gate_w': jax.random.normal(ks[6], (d, INTER * 2), jnp.float32) * s(d), 'down_w': jax.random.normal(ks[7], (INTER, d), jnp.float32) * s(INTER)}
    _L0_attn_in = _L0_attn_setup()

    def _L0_ffn_setup():
        import jax, jax.numpy as jnp
        import numpy as np

        def _sparsify_2to4(h):
            B, S, I = h.shape
            g = h.reshape(B, S, I // 4, 4)
            a = jnp.abs(g)
            _, idx = jax.lax.top_k(a, 2)
            pos = jnp.arange(4)
            mask = (pos == idx[..., 0:1]) | (pos == idx[..., 1:2])
            return (g * mask.astype(g.dtype)).reshape(B, S, I)
        key = jax.random.key(seed)
        k1, k2, k3, k4 = jax.random.split(key, 4)
        B, S, H, I = (4, 512, 512, 2048)
        x = jax.random.normal(k1, (B, S, H), dtype=jnp.float32)
        w_gate = jax.random.normal(k2, (H, I), dtype=jnp.float32) / np.sqrt(H)
        w_up = jax.random.normal(k3, (H, I), dtype=jnp.float32) / np.sqrt(H)
        w_down = jax.random.normal(k4, (I, H), dtype=jnp.float32) / np.sqrt(I)
        return {'x': x, 'w_gate': w_gate, 'w_up': w_up, 'w_down': w_down}
    _L0_ffn_in = _L0_ffn_setup()
    _d = {'L0_attn_hidden_states': _L0_attn_in['hidden_states'], 'L0_attn_attn_norm_w': _L0_attn_in['attn_norm_w'], 'L0_attn_q_w': _L0_attn_in['q_w'], 'L0_attn_k_w': _L0_attn_in['k_w'], 'L0_attn_v_w': _L0_attn_in['v_w'], 'L0_attn_g_w': _L0_attn_in['g_w'], 'L0_attn_o_w': _L0_attn_in['o_w'], 'L0_attn_gnorm_w': _L0_attn_in['gnorm_w'], 'L0_attn_mlp_norm_w': _L0_attn_in['mlp_norm_w'], 'L0_attn_gate_w': _L0_attn_in['gate_w'], 'L0_attn_down_w': _L0_attn_in['down_w'], 'L0_ffn_w_gate': _L0_ffn_in['w_gate'], 'L0_ffn_w_up': _L0_ffn_in['w_up'], 'L0_ffn_w_down': _L0_ffn_in['w_down']}
    _x0 = _d['L0_attn_hidden_states']
    _d['L0_attn_hidden_states'] = jax.random.normal(jax.random.fold_in(jax.random.key(seed), 1), (4, 1024, 512), dtype=_x0.dtype)
    del _x0
    return _d

def reference(L0_attn_hidden_states, L0_attn_attn_norm_w, L0_attn_q_w, L0_attn_k_w, L0_attn_v_w, L0_attn_g_w, L0_attn_o_w, L0_attn_gnorm_w, L0_attn_mlp_norm_w, L0_attn_gate_w, L0_attn_down_w, L0_ffn_w_gate, L0_ffn_w_up, L0_ffn_w_down):

    def _L0_attn_ref(hidden_states, attn_norm_w, q_w, k_w, v_w, g_w, o_w, gnorm_w, mlp_norm_w, gate_w, down_w):
        import jax, jax.numpy as jnp
        import numpy as np
        D_MODEL = 512
        N_HEADS = 8
        EXPAND_K = 1
        EXPAND_V = 2
        DK = D_MODEL * EXPAND_K // N_HEADS
        DV = D_MODEL * EXPAND_V // N_HEADS
        INTER = 1408
        EPS = 1e-06
        CHUNK = 64

        def rmsnorm(x, w, eps=EPS):
            return x * jax.lax.rsqrt(jnp.mean(x * x, axis=-1, keepdims=True) + eps) * w

        def rope(x):
            T, D = (x.shape[1], x.shape[-1])
            inv_freq = 1.0 / 10000.0 ** (jnp.arange(0, D, 2, dtype=jnp.float32) / D)
            ang = jnp.arange(T, dtype=jnp.float32)[:, None] * inv_freq
            cos = jnp.cos(ang)[None, :, None, :]
            sin = jnp.sin(ang)[None, :, None, :]
            x1, x2 = jnp.split(x, 2, axis=-1)
            return jnp.concatenate([x1 * cos - x2 * sin, x2 * cos + x1 * sin], axis=-1)

        def chunk_retention(q, k, v):
            B, T, H, Dk = q.shape
            Dv = v.shape[-1]
            C = CHUNK
            N = T // C
            gamma = 1.0 - jnp.exp2(-5.0 - jnp.arange(H, dtype=jnp.float32))
            i = jnp.arange(C, dtype=jnp.float32)
            diff = i[:, None] - i[None, :]
            Dmask = jnp.where(diff >= 0, gamma[:, None, None] ** diff, 0.0)
            cross_decay = gamma[:, None] ** (i[None, :] + 1.0)
            k_decay = gamma[:, None] ** (C - 1.0 - i[None, :])
            chunk_decay = gamma ** C
            to_chunks = lambda x: jnp.moveaxis(x.reshape(B, N, C, H, x.shape[-1]).transpose(0, 1, 3, 2, 4), 1, 0)
            qc, kc, vc = (to_chunks(q), to_chunks(k), to_chunks(v))

            def body(S, inp):
                qb, kb, vb = inp
                attn = jnp.einsum('bhid,bhjd->bhij', qb, kb) * Dmask
                o_intra = jnp.einsum('bhij,bhje->bhie', attn, vb)
                o_cross = jnp.einsum('bhid,bhde->bhie', qb * cross_decay[None, :, :, None], S)
                S = chunk_decay[None, :, None, None] * S + jnp.einsum('bhid,bhie->bhde', kb * k_decay[None, :, :, None], vb)
                return (S, o_intra + o_cross)
            S0 = jnp.zeros((B, H, Dk, Dv), q.dtype)
            _, o = jax.lax.scan(body, S0, (qc, kc, vc))
            return jnp.moveaxis(o, 0, 1).transpose(0, 1, 3, 2, 4).reshape(B, T, H, Dv)
        B, T, d = hidden_states.shape
        residual = hidden_states
        h = rmsnorm(hidden_states, attn_norm_w)
        q = (h @ q_w).reshape(B, T, N_HEADS, DK)
        k = (h @ k_w).reshape(B, T, N_HEADS, DK)
        v = (h @ v_w).reshape(B, T, N_HEADS, DV)
        g = (h @ g_w).reshape(B, T, N_HEADS, DV)
        q, k = (rope(q), rope(k))
        q = q * DK ** (-0.5)
        o = chunk_retention(q, k, v)
        o = rmsnorm(o, gnorm_w) * (g * jax.nn.sigmoid(g))
        h = o.reshape(B, T, N_HEADS * DV) @ o_w
        residual = h + residual
        h = rmsnorm(residual, mlp_norm_w)
        y = h @ gate_w
        gate, y = jnp.split(y, 2, axis=-1)
        h = gate * jax.nn.sigmoid(gate) * y @ down_w
        return residual + h

    def _L0_ffn_ref(x, w_gate, w_up, w_down):
        import jax, jax.numpy as jnp
        import numpy as np

        def _sparsify_2to4(h):
            B, S, I = h.shape
            g = h.reshape(B, S, I // 4, 4)
            a = jnp.abs(g)
            _, idx = jax.lax.top_k(a, 2)
            pos = jnp.arange(4)
            mask = (pos == idx[..., 0:1]) | (pos == idx[..., 1:2])
            return (g * mask.astype(g.dtype)).reshape(B, S, I)
        h = jax.nn.silu(jnp.einsum('bsh,hi->bsi', x, w_gate)) * jnp.einsum('bsh,hi->bsi', x, w_up)
        h_sparse = _sparsify_2to4(h)
        return jnp.einsum('bsi,ih->bsh', h_sparse, w_down)
    x = L0_attn_hidden_states
    x = x + _L0_attn_ref(_layernorm(x, axis=-1), L0_attn_attn_norm_w, L0_attn_q_w, L0_attn_k_w, L0_attn_v_w, L0_attn_g_w, L0_attn_o_w, L0_attn_gnorm_w, L0_attn_mlp_norm_w, L0_attn_gate_w, L0_attn_down_w)
    x = x + _L0_ffn_ref(_layernorm(x, axis=-1), L0_ffn_w_gate, L0_ffn_w_up, L0_ffn_w_down)
    return x

_drawn_inputs = setup_inputs


def setup_inputs(seed=0):
    import zlib

    import numpy as np

    out = dict(_drawn_inputs(seed))
    spreads = {'L0_attn_attn_norm_w': (1.0, 0.2),
     'L0_attn_gnorm_w': (1.0, 0.2),
     'L0_attn_mlp_norm_w': (1.0, 0.2)}
    factors = {}
    for name, (base, spread) in spreads.items():
        noise = np.random.default_rng([zlib.crc32(name.encode()), seed]).standard_normal(out[name].shape)
        drawn = base * np.exp(spread * noise) if base else spread * noise
        out[name] = jnp.asarray(drawn.astype(out[name].dtype))
    for name, factor in factors.items():
        out[name] = (out[name] * factor).astype(out[name].dtype)
    return out
```

```python
from contextlib import ExitStack

import concourse.bass as bass
from concourse import mybir

F32 = mybir.dt.float32
F32R = mybir.dt.float32r
BF16 = mybir.dt.bfloat16
ALU = mybir.AluOpType
ACT = mybir.ActivationFunctionType
AX_X = mybir.AxisListType.X

P = 128
B, L, D = 4, 1024, 512
H, DK, DV = 8, 64, 128
KC = D // P
CH = L // P
STEPS = B * CH
PAIRS = H // 2
INTER = 1408
FT = INTER // P
TOK = 512
SUB = TOK // P
TILES = B * L // TOK
HID = 2048
HALVES = 2
SETS = HID // HALVES // (4 * P)
LN_EPS, RMS_EPS = 1e-5, 1e-6

PIECE1, NP1 = 1024, 16
PIECE2, NP2 = 3 * 512, FT
PIECE3, NP3 = 1024, 6 * SETS
Q0, K0, V0, G0, O0 = 0, 2, 4, 8, 12
SLOTS = 3

COS, SIN, DEC, GAM, MASK, IDN, NCONST = 0, 512, 1024, 1040, 1552, 1680, 1808


def build_program(nc, x, attn_norm_w, q_w, k_w, v_w, g_w, o_w, gnorm_w, mlp_norm_w, gate_w, down_w,
                  f_gate_w, f_up_w, f_down_w, consts, out):
    x_rows = x.rearrange("b (c p) d -> (b c) p d", p=P)
    x_tiles = x.rearrange("b (t s p) d -> (b t) p s d", s=SUB, p=P)
    out_tiles = out.rearrange("b (t s p) d -> (b t) p s d", s=SUB, p=P)
    x2_dram = nc.dram_tensor("x2_dram", (B * L, D), F32, kind="Internal").ap()
    y_dram = nc.dram_tensor("y_dram", (B * L, D), F32, kind="Internal").ap()
    z_dram = nc.dram_tensor("z_dram", (B * L, D), F32, kind="Internal").ap()
    x2_rows = x2_dram.rearrange("(n p) d -> n p d", p=P)
    tiles_of = lambda a: a.rearrange("(t s p) d -> t p s d", s=SUB, p=P)
    x2_tiles, y_tiles, z_tiles = tiles_of(x2_dram), tiles_of(y_dram), tiles_of(z_dram)

    with ExitStack() as ctx:
        def sem(name):
            return ctx.enter_context(nc.semaphore(name))

        def sb(stack, name, shape, dt=F32):
            return stack.enter_context(nc.sbuf_tensor(name, shape, dt))

        ps = ctx.enter_context(nc.psum_tensor("ps", [P, 8, 512], F32))

        stage = sb(ctx, "stage", [P, SLOTS, PIECE2])
        idn = sb(ctx, "idn", [P, P])
        norms = sb(ctx, "norms", [P, 2 * KC + 1])
        pool_c = sb(ctx, "pool_c", [P, 3, 8])
        ident = idn[:]

        with ExitStack() as c1:
            W1h = sb(c1, "W1h", [P, NP1, PIECE1], F32R)
            W1l = sb(c1, "W1l", [P, NP1, PIECE1], F32R)
            tab = sb(c1, "tab", [P, IDN])
            xt = sb(c1, "xt", [P, D])
            x1 = sb(c1, "x1", [P, 2, D])
            hTh = sb(c1, "hTh", [P, KC, P], F32R)
            hTl = sb(c1, "hTl", [P, KC, P], F32R)
            rc = sb(c1, "rc", [P, 2 * H, DK])
            rs = sb(c1, "rs", [P, 2 * H, DK])
            rc_flat, rs_flat = (a[:].rearrange("p h d -> p (h d)") for a in (rc, rs))
            kT = rc_flat[:, 0:PAIRS * P].rearrange("p (r j) -> p r j", r=PAIRS)
            x2 = rc_flat[:, PAIRS * P:PAIRS * P + D]
            h = rs_flat[:, 0:D]
            qk = sb(c1, "qk", [P, 2 * H, DK])
            qbd = sb(c1, "qbd", [P, PAIRS, 2, P])
            sc = sb(c1, "sc", [P, H, P])
            v = sb(c1, "v", [P, H, DV])
            sg = sb(c1, "sg", [P, H, DV])
            onTh = sb(c1, "onTh", [P, H, P], F32R)
            onTl = sb(c1, "onTl", [P, H, P], F32R)
            state = sb(c1, "state", [P, B, PAIRS * DV])
            st = sb(c1, "st", [P, 8])
            mv = sb(c1, "mv", [P, 2])
            nrm = sb(c1, "nrm", [P, 6])
            oss = sb(c1, "oss", [P, H])
            ome = sb(c1, "ome", [P, H])
            ors = sb(c1, "ors", [P, H])
        with ExitStack() as c2:
            W2h = sb(c2, "W2h", [P, NP2, PIECE2], F32R)
            W2l = sb(c2, "W2l", [P, NP2, PIECE2], F32R)
            h2Th = sb(c2, "h2Th", [P, KC, TOK], F32R)
            h2Tl = sb(c2, "h2Tl", [P, KC, TOK], F32R)
            x2t = sb(c2, "x2t", [P, SUB, D])
            h2 = sb(c2, "h2", [P, SUB, D])
            res = sb(c2, "res", [P, SUB, D])
            sg2 = sb(c2, "sg2", [P, 2, TOK])
            u2 = sb(c2, "u2", [P, 2, TOK])
            u2h = sb(c2, "u2h", [P, 2, TOK], F32R)
            u2l = sb(c2, "u2l", [P, 2, TOK], F32R)
            ssq = sb(c2, "ssq", [P, SUB])
            sme = sb(c2, "sme", [P, SUB])
            srs = sb(c2, "srs", [P, SUB])
        with ExitStack() as c3:
            W3h = sb(c3, "W3h", [P, NP3, PIECE3], F32R)
            W3l = sb(c3, "W3l", [P, NP3, PIECE3], F32R)
            xnTh = sb(c3, "xnTh", [P, KC, TOK], F32R)
            xnTl = sb(c3, "xnTl", [P, KC, TOK], F32R)
            yt = sb(c3, "yt", [P, SUB, D])
            xn = sb(c3, "xn", [P, SUB, D])
            acc = sb(c3, "acc", [P, SUB, D])
            sg3 = sb(c3, "sg3", [P, 2, TOK])
            hh = sb(c3, "hh", [P, 4, TOK])
            ab = sb(c3, "ab", [P, 4, TOK])
            cmp = sb(c3, "cmp", [P, 6, TOK], BF16)
            win = sb(c3, "win", [P, 4, TOK], BF16)
            u3h = sb(c3, "u3h", [P, 4, TOK], F32R)
            u3l = sb(c3, "u3l", [P, 4, TOK], F32R)
            st3 = sb(c3, "st3", [P, SUB, 6])
            mv3 = sb(c3, "mv3", [P, SUB, 2])
            ve3 = sb(c3, "ve3", [P, SUB])
            rs3 = sb(c3, "rs3", [P, SUB])

        consts_in = sem("consts_in")
        pool_c_set = sem("pool_c_set")
        staged = [sem(f"staged{i}") for i in range(SLOTS)]
        w_hi = sem("w_hi")
        w_lo = sem("w_lo")
        x_in = sem("x_in")
        stat = sem("stat")
        mean_var = sem("mean_var")
        nrm_chain = sem("nrm_chain")
        rstd_ok = sem("rstd_ok")
        x1_ok = sem("x1_ok")
        h_ok = sem("h_ok")
        hT_ps = sem("hT_ps")
        hT_hi = sem("hT_hi")
        hT_lo = sem("hT_lo")
        qk_ps = sem("qk_ps")
        rope_prod = sem("rope_prod")
        rope_sum = sem("rope_sum")
        qk_ok = sem("qk_ok")
        qkT_ps = sem("qkT_ps")
        kT_ok = sem("kT_ok")
        qT_ok = sem("qT_ok")
        qbd_zero = sem("qbd_zero")
        v_ps = sem("v_ps")
        v_ok = sem("v_ok")
        g_ps = sem("g_ps")
        sg_ok = sem("sg_ok")
        s_ps = sem("s_ps")
        s_ok = sem("s_ok")
        o_ps = sem("o_ps")
        osq_ok = sem("osq_ok")
        oss_ok = sem("oss_ok")
        ome_ok = sem("ome_ok")
        ors_ok = sem("ors_ok")
        og_ok = sem("og_ok")
        on_ok = sem("on_ok")
        onT_ps = sem("onT_ps")
        onT_hi = sem("onT_hi")
        onT_lo = sem("onT_lo")
        attn_ps = sem("attn_ps")
        x2_ok = sem("x2_ok")
        x2_out = sem("x2_out")
        u_ps = sem("u_ps")
        state_sum = sem("state_sum")
        state_ok = sem("state_ok")
        x2t_in = sem("x2t_in")
        xres_in = sem("xres_in")
        res_ok = sem("res_ok")
        ssq_ok = sem("ssq_ok")
        sme_ok = sem("sme_ok")
        srs_ok = sem("srs_ok")
        h2_ok = sem("h2_ok")
        h2T_ps = sem("h2T_ps")
        h2T_hi = sem("h2T_hi")
        h2T_lo = sem("h2T_lo")
        up2_ps = sem("up2_ps")
        sg2_ok = sem("sg2_ok")
        u2_ok = sem("u2_ok")
        u2_hi = sem("u2_hi")
        u2_lo = sem("u2_lo")
        down2 = sem("down2")
        y_ok = sem("y_ok")
        y_out = sem("y_out")
        yt_in = sem("yt_in")
        st3_ok = sem("st3_ok")
        mv3_ok = sem("mv3_ok")
        ve3_ok = sem("ve3_ok")
        rs3_ok = sem("rs3_ok")
        xn_ok = sem("xn_ok")
        xnT_ps = sem("xnT_ps")
        xnT_hi = sem("xnT_hi")
        xnT_lo = sem("xnT_lo")
        up3_ps = sem("up3_ps")
        sg3_ok = sem("sg3_ok")
        hh_ok = sem("hh_ok")
        ab_ok = sem("ab_ok")
        cmp_ok = sem("cmp_ok")
        win_ok = sem("win_ok")
        win2_ok = sem("win2_ok")
        kept = sem("kept")
        u3_hi = sem("u3_hi")
        u3_lo = sem("u3_lo")
        down3 = sem("down3")
        acc_in = sem("acc_in")
        acc_ok = sem("acc_ok")
        acc_out = sem("acc_out")

        def rows2(w, j, cols=slice(None)):
            return w.rearrange("(a p) n -> p a n", p=P)[:, 2 * j:2 * j + 2, cols]

        def pieces():
            for name, first in (("q", Q0), ("k", K0)):
                w = q_w if name == "q" else k_w
                for j in range(2):
                    yield ([(0, rows2(w, j))], [(512 * a, 512, 2 * j + a) for a in range(2)], 1, first + j)
            for w, first in ((v_w, V0), (g_w, G0)):
                for kc in range(KC):
                    yield ([(0, w.rearrange("(a p) n -> p a n", p=P)[:, kc:kc + 1, :])],
                           [(0, 1024, kc)], 1, first + kc)
            for j in range(4):
                yield [(0, rows2(o_w, j))], [(0, 1024, 2 * KC)], 1, O0 + j
            gate = gate_w.rearrange("(a p) n -> p a n", p=P)
            down = down_w.rearrange("(f p) n -> p f n", p=P)
            for f in range(FT):
                loads = [(0, gate[:, :, f * P:f * P + P]), (512, gate[:, :, INTER + f * P:INTER + f * P + P]),
                         (1024, down[:, f:f + 1, :])]
                parts = [(512 * g + P * kc, P, KC + kc) for kc in range(KC) for g in range(2)]
                yield loads, parts + [(1024, 512, None)], 2, f
            fdown = f_down_w.rearrange("(g p r) n -> g p r n", p=P, r=4)
            for half in range(HALVES):
                for s in range(SETS):
                    c0 = (half * SETS + s) * 512
                    for w, k in ((f_gate_w, 0), (f_up_w, 2)):
                        for j in range(2):
                            yield [(0, rows2(w, j, slice(c0, c0 + 512)))], "group", 3, 4 * s + k + j
                for s in range(SETS):
                    for j in range(2):
                        yield ([(0, fdown[half * SETS + s][:, 2 * j:2 * j + 2, :])],
                               [(0, 1024, None)], 3, 4 * SETS + 2 * s + j)

        PIECES = list(pieces())
        ENDS = [NP1, NP1 + NP2, NP1 + NP2 + NP3, NP1 + NP2 + 2 * NP3]
        hi_of = {1: W1h, 2: W2h, 3: W3h}
        lo_of = {1: W1l, 2: W2l, 3: W3l}
        loads_before = [sum(len(PIECES[m][0]) for m in range(n + 1) if m % SLOTS == n % SLOTS)
                        for n in range(len(PIECES))]

        def need(eng, s, n):
            if not isinstance(n, int) or n > 0:
                eng.wait_ge(s, n)

        def load_piece(eng, n):
            loads, parts, phase, at = PIECES[n]
            need(eng, w_lo, n - SLOTS + 1)
            for col, src in loads:
                width = src.shape[1] * src.shape[2]
                dst = stage[:, n % SLOTS, col:col + width].rearrange("p (a n) -> p a n", a=src.shape[1])
                eng.dma_start(dst, src).then_inc(staged[n % SLOTS], 16)

        def split_piece(eng, n, hi):
            loads, parts, phase, at = PIECES[n]
            raw, dh, dl = stage[:, n % SLOTS], hi_of[phase][:, at], lo_of[phase][:, at]
            eng.wait_ge(staged[n % SLOTS], 16 * loads_before[n])
            if not hi:
                eng.wait_ge(w_hi, n + 1)
            if parts == "group":
                for a in range(2):
                    src = raw[:, 512 * a:512 * a + 512].rearrange("p (g r) -> p r g", r=4)
                    to = (dh if hi else dl)[:, 512 * a:512 * a + 512].rearrange("p (r g) -> p r g", r=4)
                    if hi:
                        ins = eng.copy(to, src)
                    else:
                        got = dh[:, 512 * a:512 * a + 512].bitcast(F32).rearrange("p (r g) -> p r g", r=4)
                        ins = eng.tensor_tensor(to, src, got, ALU.subtract)
            else:
                for col, width, norm in parts:
                    cut = slice(col, col + width)
                    scale = norms[:, norm:norm + 1] if norm is not None else 1.0
                    if hi:
                        ins = eng.activation(dh[:, cut], raw[:, cut], ACT.Copy, scale=scale)
                    else:
                        ins = eng.scalar_tensor_tensor(out=dl[:, cut], in0=raw[:, cut], scalar=scale,
                                                       in1=dh[:, cut].bitcast(F32), op0=ALU.mult,
                                                       op1=ALU.subtract)
            ins.then_inc(w_hi if hi else w_lo, 1)

        def mm3(pe, dst, lh, ll, rh, rl, start, stop):
            pe.matmul(dst, lh, rh, start=start, stop=False)
            pe.matmul(dst, lh, rl, start=False, stop=False)
            return pe.matmul(dst, ll, rh, start=False, stop=stop)

        def row_tile(t):
            return (t % B) * CH + t // B

        def tile_at(a, i):
            return a[bass.ds(i, 1)].rearrange("a p s d -> p (a s) d")

        block = ctx.enter_context(nc.Block())

        @block.sync
        def _(sp):
            sp.dma_start(xt[:], x_rows[row_tile(0)]).then_inc(x_in, 16)
            sp.dma_start(tab[:], consts[:, 0:IDN]).then_inc(consts_in, 16)
            sp.dma_start(idn[:], consts[:, IDN:IDN + P]).then_inc(consts_in, 16)
            sp.dma_start(norms[:, 0:KC], attn_norm_w.rearrange("(k p) -> p k", p=P), allow_slow_non_contiguous=True).then_inc(consts_in, 16)
            sp.dma_start(norms[:, KC:2 * KC], mlp_norm_w.rearrange("(k p) -> p k", p=P), allow_slow_non_contiguous=True).then_inc(consts_in, 16)
            sp.dma_start(norms[:, 2 * KC:2 * KC + 1], gnorm_w.rearrange("(p k) -> p k", k=1), allow_slow_non_contiguous=True).then_inc(consts_in, 16)
            for n in range(4):
                load_piece(sp, n)
            sp.wait_ge(x1_ok, 1)
            sp.dma_start(xt[:], x_rows[row_tile(1)]).then_inc(x_in, 16)
            for n in range(4, NP1):
                load_piece(sp, n)

            def row_at(a, t):
                return a[bass.ds(row_tile(t), 1)].rearrange("a p d -> p (a d)")

            def load_x(t):
                sp.wait_ge(x1_ok, t)
                sp.dma_start(xt[:], row_at(x_rows, t)).then_inc(x_in, 16)

            def store_x2(t):
                sp.wait_ge(x2_ok, t + 1)
                sp.dma_start(row_at(x2_rows, t), x2).then_inc(x2_out, 16)

            sp.wait_ge(x1_ok, 2)
            sp.dma_start(xt[:], x_rows[row_tile(2)]).then_inc(x_in, 16)
            with sp.Fori(0, STEPS - 3) as t:
                store_x2(t)
                load_x(t + 3)
            for t in range(STEPS - 3, STEPS):
                if t == STEPS - 1:
                    for n in range(NP1, NP1 + SLOTS):
                        load_piece(sp, n)
                sp.wait_ge(x2_ok, t + 1)
                sp.dma_start(x2_rows[row_tile(t)], x2).then_inc(x2_out, 16)

            sp.wait_ge(x2_out, 16 * STEPS)
            sp.wait_ge(attn_ps, STEPS)
            sp.dma_start(x2t[:], x2_tiles[0]).then_inc(x2t_in, 16)
            sp.dma_start(res[:], x_tiles[0]).then_inc(xres_in, 16)
            for n in range(NP1 + SLOTS, ENDS[1]):
                load_piece(sp, n)

            def loads2(t):
                sp.wait_ge(res_ok, t + 1)
                sp.dma_start(x2t[:], x2_tiles[t + 1]).then_inc(x2t_in, 16)

            loads2(0)
            with sp.Fori(3, TILES + 1) as i:
                sp.wait_ge(y_ok, SUB * (i - 2))
                sp.dma_start(tile_at(y_tiles, i - 3), res[:]).then_inc(y_out, 16)
                sp.wait_ge(y_out, 16 * (i - 2))
                sp.dma_start(res[:], tile_at(x_tiles, i - 2)).then_inc(xres_in, 16)
                sp.wait_ge(res_ok, i - 1)
                sp.dma_start(x2t[:], tile_at(x2_tiles, i - 1)).then_inc(x2t_in, 16)
            t = TILES - 2
            sp.wait_ge(y_ok, SUB * (t + 1))
            sp.dma_start(y_tiles[t], res[:]).then_inc(y_out, 16)
            sp.wait_ge(y_out, 16 * (t + 1))
            sp.dma_start(res[:], x_tiles[t + 1]).then_inc(xres_in, 16)
            for n in range(ENDS[1], ENDS[1] + SLOTS):
                load_piece(sp, n)
            sp.wait_ge(y_ok, SUB * TILES)
            sp.dma_start(y_tiles[TILES - 1], res[:]).then_inc(y_out, 16)

            sp.wait_ge(y_out, 16 * TILES)
            sp.wait_ge(down2, FT * TILES)
            for half in range(HALVES):
                t0 = half * TILES
                src, dst = (y_tiles, z_tiles) if half == 0 else (z_tiles, out_tiles)
                if half:
                    sp.wait_ge(acc_out, 16 * t0)
                    sp.wait_ge(xn_ok, SUB * t0)
                sp.dma_start(yt[:], y_tiles[0]).then_inc(yt_in, 16)
                for n in range(ENDS[1 + half] + (SLOTS if half == 0 else 0), ENDS[2 + half]):
                    load_piece(sp, n)
                sp.wait_ge(xn_ok, SUB * (t0 + 1))
                sp.dma_start(yt[:], y_tiles[1]).then_inc(yt_in, 16)
                sp.dma_start(acc[:], src[0]).then_inc(acc_in, 16)
                with sp.Fori(3, TILES + 1) as i:
                    sp.wait_ge(xn_ok, SUB * (i - 1 + t0))
                    sp.dma_start(yt[:], tile_at(y_tiles, i - 1)).then_inc(yt_in, 16)
                    sp.wait_ge(acc_ok, SUB * (i - 2 + t0))
                    sp.dma_start(tile_at(dst, i - 3), acc[:]).then_inc(acc_out, 16)
                    sp.wait_ge(acc_out, 16 * (i - 2 + t0))
                    sp.dma_start(acc[:], tile_at(src, i - 2)).then_inc(acc_in, 16)
                for t in (TILES - 2, TILES - 1):
                    sp.wait_ge(acc_ok, SUB * (t0 + t + 1))
                    sp.dma_start(dst[t], acc[:]).then_inc(acc_out, 16)
                    sp.wait_ge(acc_out, 16 * (t0 + t + 1))
                    if t == TILES - 2:
                        sp.dma_start(acc[:], src[t + 1]).then_inc(acc_in, 16)

        @block.gpsimd
        def _(pool):
            for at, value in enumerate((-0.5, LN_EPS, RMS_EPS)):
                pool.memset(pool_c[:, at], value).then_inc(pool_c_set, 1)
            pool.memset(qbd[:], 0.0).then_inc(qbd_zero, 1)
            pool.wait_ge(pool_c_set, 3)
            minus_half, ln_eps, rms_eps = (pool_c[:, at] for at in range(3))

            def norm_scalars(t):
                var, ve, rstd, vr, vrr, vrre, r2 = mv[:, 1:2], *(nrm[:, i:i + 1] for i in range(6))
                pool.wait_ge(mean_var, t + 1)
                need(pool, h_ok, t)
                pool.tensor_tensor(ve, var, ln_eps[:, 0:1], ALU.add).then_inc(nrm_chain, 1)
                pool.wait_ge(nrm_chain, 4 * t + 1)
                pool.tensor_tensor(rstd, ve, minus_half[:, 0:1], ALU.pow).then_inc(rstd_ok, 1)
                pool.wait_ge(rstd_ok, 2 * t + 1)
                pool.tensor_tensor(vr, var, rstd, ALU.mult).then_inc(nrm_chain, 1)
                pool.wait_ge(nrm_chain, 4 * t + 2)
                pool.tensor_tensor(vrr, vr, rstd, ALU.mult).then_inc(nrm_chain, 1)
                pool.wait_ge(nrm_chain, 4 * t + 3)
                pool.tensor_tensor(vrre, vrr, rms_eps[:, 0:1], ALU.add).then_inc(nrm_chain, 1)
                pool.wait_ge(nrm_chain, 4 * t + 4)
                pool.tensor_tensor(r2, vrre, minus_half[:, 0:1], ALU.pow).then_inc(rstd_ok, 1)

            def head_scalars(t):
                pool.wait_ge(oss_ok, t + 1)
                pool.tensor_tensor(ome[:], oss[:], rms_eps, ALU.add).then_inc(ome_ok, 1)
                pool.wait_ge(ome_ok, t + 1)
                pool.tensor_tensor(ors[:], ome[:], minus_half, ALU.pow).then_inc(ors_ok, 1)

            norm_scalars(0)
            norm_scalars(1)
            head_scalars(0)
            with pool.Fori(1, STEPS - 1) as t:
                norm_scalars(t + 1)
                head_scalars(t)
            head_scalars(STEPS - 1)

            pool.wait_ge(x2_out, 16 * STEPS)
            pool.wait_ge(attn_ps, STEPS)

            def rms_scalars(t):
                pool.wait_ge(ssq_ok, SUB * t + SUB)
                pool.tensor_tensor(sme[:], ssq[:], rms_eps[:, 0:SUB], ALU.add).then_inc(sme_ok, 1)
                pool.wait_ge(sme_ok, t + 1)
                pool.tensor_tensor(srs[:], sme[:], minus_half[:, 0:SUB], ALU.pow).then_inc(srs_ok, 1)

            def residual(t):
                pool.wait_ge(xres_in, 16 * t + 16)
                pool.wait_ge(x2t_in, 16 * t + 16)
                pool.wait_ge(h2_ok, SUB * t + SUB)
                pool.tensor_tensor(res[:], res[:], x2t[:], ALU.add).then_inc(res_ok, 1)

            rms_scalars(0)
            residual(0)
            with pool.Fori(1, TILES) as t:
                rms_scalars(t)
                residual(t)

            pool.wait_ge(y_out, 16 * TILES)
            pool.wait_ge(down2, FT * TILES)
            with pool.Fori(0, HALVES * TILES) as t:
                pool.wait_ge(mv3_ok, SUB * t + SUB)
                pool.tensor_tensor(ve3[:], mv3[:, :, 1], ln_eps[:, 0:SUB], ALU.add).then_inc(ve3_ok, 1)
                pool.wait_ge(ve3_ok, t + 1)
                pool.tensor_tensor(rs3[:], ve3[:], minus_half[:, 0:SUB], ALU.pow).then_inc(rs3_ok, 1)

        @block.scalar
        def _(act):
            def make_h(t):
                act.wait_ge(x1_ok, t + 1)
                act.wait_ge(rstd_ok, 2 * t + 2)
                slot = x1[:, t % 2] if isinstance(t, int) else x1[:, bass.ds(t % 2, 1)].rearrange("p a d -> p (a d)")
                act.activation(h, slot, ACT.Copy, scale=nrm[:, 5:6]).then_inc(h_ok, 1)

            def hT_round(t):
                act.wait_ge(hT_ps, t + 1)
                act.copy(hTh[:].rearrange("p k t -> p (k t)"), ps[:, 7]).then_inc(hT_hi, 1)

            def onT_round(t):
                for j in range(2):
                    act.wait_ge(onT_ps, 2 * t + j + 1)
                    act.copy(onTh[:, 4 * j:4 * j + 4].rearrange("p h t -> p (h t)"), ps[:, 4 + j]).then_inc(onT_hi, 1)

            def step(t, first, last):
                if not first:
                    for j in range(2):
                        act.wait_ge(onT_ps, 2 * t + j - 1)
                        act.copy(onTh[:, 4 * j:4 * j + 4].rearrange("p h t -> p (h t)"), ps[:, 4 + j]).then_inc(onT_hi, 1)
                act.wait_ge(v_ps, t + 1)
                act.copy(v[:].rearrange("p h e -> p (h e)"), ps[:, 2:4].rearrange("p a n -> p (a n)")).then_inc(v_ok, 1)
                act.wait_ge(qkT_ps, 2 * t + 1)
                qT = ps[:, 0].rearrange("p (r i) -> p r i", r=PAIRS)
                if first:
                    act.wait_ge(qbd_zero, 1)
                act.copy(qbd[0:64, :, 0], qT[0:64]).then_inc(qT_ok, 1)
                act.copy(qbd[64:128, :, 1], qT[64:128]).then_inc(qT_ok, 1)
                act.wait_ge(qkT_ps, 2 * t + 2)
                act.copy(kT.rearrange("p r j -> p (r j)"), ps[:, 1]).then_inc(kT_ok, 1)
                act.wait_ge(g_ps, 2 * t + 1)
                act.activation(sg[:, 0:4].rearrange("p h e -> p (h e)"), ps[:, 4], ACT.Silu).then_inc(sg_ok, 1)
                if not last:
                    make_h(t + 1)
                act.wait_ge(g_ps, 2 * t + 2)
                act.activation(sg[:, 4:8].rearrange("p h e -> p (h e)"), ps[:, 5], ACT.Silu).then_inc(sg_ok, 1)
                if not last:
                    hT_round(t + 1)
                act.wait_ge(o_ps, t + 1)
                act.activation(rs[:].rearrange("p h e -> p (h e)"), ps[:, 2:4].rearrange("p a n -> p (a n)"),
                               ACT.Square, scale=DV ** -0.5).then_inc(osq_ok, 1)

            act.wait_ge(consts_in, 80)
            for n in range(2):
                split_piece(act, n, True)
            make_h(0)
            hT_round(0)
            for n in range(2, NP1):
                split_piece(act, n, True)
            step(0, True, False)
            with act.Fori(1, STEPS - 1) as t:
                step(t, False, False)
            step(STEPS - 1, False, True)
            onT_round(STEPS - 1)

            def square_x2(t):
                act.wait_ge(x2t_in, 16 * t + 16)
                for s in range(SUB):
                    act.activation(h2[:, s], x2t[:, s], ACT.Square, scale=D ** -0.5,
                                   accum_out=ssq[:, s:s + 1]).then_inc(ssq_ok, 1)

            def make_h2(t):
                act.wait_ge(srs_ok, t + 1)
                for s in range(SUB):
                    act.activation(h2[:, s], x2t[:, s], ACT.Copy, scale=srs[:, s:s + 1]).then_inc(h2_ok, 1)

            def h2T_round(t):
                for k, bank in enumerate((6, 7, 4, 5)):
                    act.wait_ge(h2T_ps, KC * t + k + 1)
                    act.copy(h2Th[:, k], ps[:, bank]).then_inc(h2T_hi, 1)

            def tile2(t, last):
                for f in range(FT):
                    act.wait_ge(up2_ps, FT * t + f + 1)
                    act.activation(sg2[:, f % 2], ps[:, 4 + 2 * (f % 2)], ACT.Silu).then_inc(sg2_ok, 1)
                    act.wait_ge(u2_ok, FT * t + f + 1)
                    if f >= 2:
                        act.wait_ge(down2, FT * t + f - 1)
                    act.copy(u2h[:, f % 2], u2[:, f % 2]).then_inc(u2_hi, 1)
                    if not last and f == 5:
                        square_x2(t + 1)
                    if not last and f == 6:
                        make_h2(t + 1)
                if not last:
                    h2T_round(t + 1)

            for n in range(NP1, NP1 + 2):
                if n == NP1:
                    act.wait_ge(attn_ps, STEPS)
                    act.wait_ge(x2_out, 16 * STEPS)
                split_piece(act, n, True)
            square_x2(0)
            make_h2(0)
            h2T_round(0)
            for n in range(NP1 + 2, ENDS[1]):
                split_piece(act, n, True)
            with act.Fori(0, TILES - 1) as t:
                tile2(t, False)
            tile2(TILES - 1, True)

            def xnT_round(t):
                for k in range(KC):
                    act.wait_ge(xnT_ps, KC * t + k + 1)
                    act.copy(xnTh[:, k], ps[:, 4 + k]).then_inc(xnT_hi, 1)

            def tile3(t, t0_first, last):
                for s in range(SETS):
                    n = SETS * t + s
                    for m in range(4):
                        act.wait_ge(up3_ps, 4 * n + m + 1)
                        act.activation(sg3[:, m % 2], ps[:, 4 + 2 * (m % 2)], ACT.Silu).then_inc(sg3_ok, 1)
                        act.wait_ge(hh_ok, 4 * n + m + 1)
                        act.activation(ab[:, m], hh[:, m], ACT.Abs).then_inc(ab_ok, 1)
                    if s == 1 and not last:
                        xnT_round(t + 1)
                    act.wait_ge(kept, 4 * n + 4)
                    if not (t0_first and s == 0 and isinstance(t, int) and t == 0):
                        act.wait_ge(down3, n)
                    act.copy(u3h[:], hh[:]).then_inc(u3_hi, 1)

            for half in range(HALVES):
                t0, n0 = half * TILES, ENDS[1 + half]
                if half == 0:
                    act.wait_ge(y_out, 16 * TILES)
                act.wait_ge(down2, FT * TILES)
                need(act, down3, SETS * t0)
                for n in range(n0, n0 + 4):
                    split_piece(act, n, True)
                xnT_round(t0)
                for n in range(n0 + 4, n0 + NP3):
                    split_piece(act, n, True)
                tile3(t0, True, False)
                with act.Fori(t0 + 1, t0 + TILES - 1) as t:
                    tile3(t, False, False)
                tile3(t0 + TILES - 1, False, True)

        @block.vector
        def _(dve):
            def x1_slot(t):
                return x1[:, t % 2] if isinstance(t, int) else x1[:, bass.ds(t % 2, 1)].rearrange("p a d -> p (a d)")

            def stats(t):
                dve.wait_ge(x_in, 16 * t + 16)
                dve.bn_stats(st[:, 0:6], xt[:]).then_inc(stat, 1)

            def aggregate():
                dve.bn_aggr(mv[:], st[:, 0:6]).then_inc(mean_var, 1)

            def make_x1(t):
                dve.wait_ge(rstd_ok, 2 * t + 1)
                dve.tensor_scalar(x1_slot(t), xt[:], mv[:, 0:1], nrm[:, 1:2], ALU.subtract,
                                  ALU.mult).then_inc(x1_ok, 1)

            def hT_rest(t):
                dve.wait_ge(hT_hi, t + 1)
                dve.tensor_tensor(hTl[:].rearrange("p k t -> p (k t)"), ps[:, 7],
                                  hTh[:].rearrange("p k t -> p (k t)").bitcast(F32), ALU.subtract).then_inc(hT_lo, 1)

            def onT_rest(n):
                for j in range(2):
                    dve.wait_ge(onT_hi, n - 1 + j if isinstance(n, int) else n + (j - 1))
                    dve.tensor_tensor(onTl[:, 4 * j:4 * j + 4].rearrange("p h t -> p (h t)"), ps[:, 4 + j],
                                      onTh[:, 4 * j:4 * j + 4].rearrange("p h t -> p (h t)").bitcast(F32),
                                      ALU.subtract).then_inc(onT_lo, 1)

            def add_residual(t, made):
                dve.wait_ge(qk_ok, made + 1 if made < STEPS else made)
                dve.wait_ge(attn_ps, made)
                dve.tensor_tensor(x2, x1_slot(t), ps[:, 6], ALU.add).then_inc(x2_ok, 1)

            def step(t, first, last):
                prev = t - 1 if isinstance(t, int) else None
                c = t // B
                dve.wait_ge(qk_ps, t + 1)
                qkp = ps[:, 0:2].rearrange("p a (h d) -> p (a h) d", d=DK)
                cos = tab[:, COS:COS + CH * DK].rearrange("p (c d) -> p c d", d=DK)[:, bass.ds(c, 1), :]
                sin = tab[:, SIN:SIN + CH * DK].rearrange("p (c d) -> p c d", d=DK)[:, bass.ds(c, 1), :]
                hd = DK // 2
                if not isinstance(t, int) or t > 1:
                    dve.wait_ge(x2_out, 16 * (t - 1))
                dve.tensor_tensor(rc[:], qkp, cos.broadcast_to([P, 2 * H, DK]), ALU.mult).then_inc(rope_prod, 1)
                dve.tensor_tensor(rs[:, :, 0:hd], qkp[:, :, hd:DK],
                                  sin[:, :, 0:hd].broadcast_to([P, 2 * H, hd]), ALU.mult).then_inc(rope_prod, 1)
                dve.tensor_tensor(rs[:, :, hd:DK], qkp[:, :, 0:hd],
                                  sin[:, :, hd:DK].broadcast_to([P, 2 * H, hd]), ALU.mult).then_inc(rope_prod, 1)
                if not first:
                    onT_rest(2 * t)
                dve.wait_ge(rope_prod, 3 * t + 3)
                dve.tensor_tensor(rc[:], rc[:], rs[:], ALU.add).then_inc(rope_sum, 1)
                if not last:
                    stats(t + 1)
                    dve.wait_ge(stat, t + 2)
                dve.wait_ge(rope_sum, t + 1)
                dve.tensor_tensor(qk[:], rc[:], tab[:, DEC:DEC + 2 * H].rearrange("p (h a) -> p h a", a=1)
                                  .broadcast_to([P, 2 * H, DK]), ALU.mult).then_inc(qk_ok, 1)
                if not last:
                    aggregate()
                if not first:
                    if isinstance(t, int):
                        add_residual(t - 1, t)
                    else:
                        add_residual_prev(t)
                if not last:
                    need(dve, x2_ok, t)
                    make_x1(t + 1)
                dve.wait_ge(s_ps, t + 1)
                dve.tensor_tensor(sc[:], ps[:, 0:2].rearrange("p a (h i) -> p (a h) i", i=P),
                                  tab[:, MASK:MASK + P].rearrange("p (a i) -> p a i", a=1).broadcast_to([P, H, P]),
                                  ALU.mult).then_inc(s_ok, 1)
                if not last:
                    hT_rest(t + 1)
                dve.wait_ge(osq_ok, t + 1)
                dve.tensor_reduce(oss[:], rs[:].rearrange("p a d -> p (a d)").rearrange("p (h e) -> p h e", e=DV),
                                  AX_X, ALU.add).then_inc(oss_ok, 1)
                dve.wait_ge(sg_ok, 2 * t + 2)
                dve.tensor_tensor(sc[:], ps[:, 2:4].rearrange("p a (h e) -> p (a h) e", e=DV), sg[:],
                                  ALU.mult).then_inc(og_ok, 1)
                b = t % B
                sb_ = state[:, b] if isinstance(t, int) else state[:, bass.ds(b, 1)].rearrange("p a n -> p (a n)")
                dve.wait_ge(u_ps, t + 1)
                dve.tensor_tensor(sb_, sb_, ps[:, 6], ALU.add).then_inc(state_sum, 1)
                dve.wait_ge(state_sum, t + 1)
                dve.tensor_tensor(sb_, sb_, tab[:, GAM:GAM + PAIRS * DV], ALU.mult).then_inc(state_ok, 1)
                dve.wait_ge(ors_ok, t + 1)
                dve.wait_ge(og_ok, t + 1)
                dve.tensor_tensor(sc[:], sc[:], ors[:].rearrange("p (h a) -> p h a", a=1).broadcast_to([P, H, DV]),
                                  ALU.mult).then_inc(on_ok, 1)

            def add_residual_prev(t):
                slot = x1[:, bass.ds((t + 1) % 2, 1)].rearrange("p a d -> p (a d)")
                dve.wait_ge(qk_ok, t + 1)
                dve.wait_ge(attn_ps, t)
                dve.tensor_tensor(x2, slot, ps[:, 6], ALU.add).then_inc(x2_ok, 1)

            dve.memset(state[:], 0.0).then_inc(state_ok, 1)
            dve.wait_ge(consts_in, 80)
            stats(0)
            dve.wait_ge(stat, 1)
            aggregate()
            make_x1(0)
            for n in range(2):
                split_piece(dve, n, False)
            hT_rest(0)
            for n in range(2, NP1):
                split_piece(dve, n, False)
            dve.wait_ge(state_ok, 1)
            step(0, True, False)
            step(1, False, False)
            with dve.Fori(2, STEPS - 1) as t:
                step(t, False, False)
            step(STEPS - 1, False, True)
            onT_rest(2 * STEPS)
            dve.wait_ge(x2_out, 16 * (STEPS - 1))
            add_residual(STEPS - 1, STEPS)

            def h2T_rest(t):
                for k, bank in enumerate((6, 7, 4, 5)):
                    dve.wait_ge(h2T_hi, KC * t + k + 1)
                    dve.tensor_tensor(h2Tl[:, k], ps[:, bank], h2Th[:, k].bitcast(F32), ALU.subtract)\
                       .then_inc(h2T_lo, 1)

            def tile2(t, last):
                for f in range(FT):
                    dve.wait_ge(sg2_ok, FT * t + f + 1)
                    dve.tensor_tensor(u2[:, f % 2], ps[:, 5 + 2 * (f % 2)], sg2[:, f % 2], ALU.mult)\
                       .then_inc(u2_ok, 1)
                    dve.wait_ge(u2_hi, FT * t + f + 1)
                    dve.tensor_tensor(u2l[:, f % 2], u2[:, f % 2], u2h[:, f % 2].bitcast(F32), ALU.subtract)\
                       .then_inc(u2_lo, 1)
                if not last:
                    h2T_rest(t + 1)
                dve.wait_ge(down2, FT * t + FT)
                dve.wait_ge(res_ok, t + 1)
                for s in range(SUB):
                    dve.tensor_tensor(res[:, s], res[:, s], ps[:, s], ALU.add).then_inc(y_ok, 1)

            dve.wait_ge(x2_out, 16 * STEPS)
            for n in range(NP1, NP1 + 2):
                split_piece(dve, n, False)
            h2T_rest(0)
            for n in range(NP1 + 2, ENDS[1]):
                split_piece(dve, n, False)
            with dve.Fori(0, TILES - 1) as t:
                tile2(t, False)
            tile2(TILES - 1, True)

            def stats3(t):
                dve.wait_ge(yt_in, 16 * t + 16)
                for s in range(SUB):
                    dve.bn_stats(st3[:, s], yt[:, s]).then_inc(st3_ok, 1)
                dve.wait_ge(st3_ok, SUB * t + SUB)

            def norm3(t):
                for s in range(SUB):
                    dve.bn_aggr(mv3[:, s], st3[:, s]).then_inc(mv3_ok, 1)
                dve.wait_ge(rs3_ok, t + 1)
                for s in range(SUB):
                    dve.tensor_scalar(xn[:, s], yt[:, s], mv3[:, s, 0:1], rs3[:, s:s + 1], ALU.subtract,
                                      ALU.mult).then_inc(xn_ok, 1)

            def xnT_rest(t):
                for k in range(KC):
                    dve.wait_ge(xnT_hi, KC * t + k + 1)
                    dve.tensor_tensor(xnTl[:, k], ps[:, 4 + k], xnTh[:, k].bitcast(F32), ALU.subtract)\
                       .then_inc(xnT_lo, 1)

            def top_two(n):
                dve.wait_ge(ab_ok, 4 * n + 4)
                dve.tensor_tensor(cmp[:, 0:2], ab[:, 0:2], ab[:, 2:4], ALU.is_ge).then_inc(cmp_ok, 1)
                dve.tensor_tensor(cmp[:, 2], ab[:, 0], ab[:, 3], ALU.is_ge).then_inc(cmp_ok, 1)
                dve.tensor_tensor(cmp[:, 3], ab[:, 1], ab[:, 2], ALU.is_ge).then_inc(cmp_ok, 1)
                dve.tensor_tensor(cmp[:, 4], ab[:, 0], ab[:, 1], ALU.is_ge).then_inc(cmp_ok, 1)
                dve.tensor_tensor(cmp[:, 5], ab[:, 2], ab[:, 3], ALU.is_ge).then_inc(cmp_ok, 1)
                dve.wait_ge(cmp_ok, 5 * n + 5)
                dve.tensor_tensor(win[:, 0:2], cmp[:, 0:2], cmp[:, 2:4], ALU.add).then_inc(win_ok, 1)
                dve.tensor_tensor(win[:, 2], cmp[:, 0], cmp[:, 3], ALU.add).then_inc(win_ok, 1)
                dve.tensor_tensor(win[:, 3], cmp[:, 1], cmp[:, 2], ALU.add).then_inc(win_ok, 1)
                dve.wait_ge(win_ok, 3 * n + 3)
                for m, other, op in ((0, 4, ALU.add), (1, 4, ALU.subtract), (2, 5, ALU.subtract), (3, 5, ALU.add)):
                    dve.tensor_tensor(win[:, m], win[:, m], cmp[:, other], op).then_inc(win2_ok, 1)
                dve.wait_ge(win2_ok, 4 * n + 4)
                for m, op, bound in ((0, ALU.is_ge, 2.0), (1, ALU.is_ge, 1.0), (2, ALU.is_le, 0.0), (3, ALU.is_le, 1.0)):
                    dve.scalar_tensor_tensor(out=hh[:, m], in0=win[:, m], scalar=bound, in1=hh[:, m], op0=op,
                                             op1=ALU.mult).then_inc(kept, 1)

            def add_down(t, made):
                dve.wait_ge(down3, made)
                dve.wait_ge(acc_in, t)
                for s in range(SUB):
                    dve.tensor_tensor(acc[:, s], acc[:, s], ps[:, s], ALU.add).then_inc(acc_ok, 1)

            def tile3(t, first, last):
                for s in range(SETS):
                    n = SETS * t + s
                    need(dve, u3_lo, n)
                    for m in range(4):
                        dve.wait_ge(sg3_ok, 4 * n + m + 1)
                        dve.tensor_tensor(hh[:, m], ps[:, 5 + 2 * (m % 2)], sg3[:, m % 2], ALU.mult)\
                           .then_inc(hh_ok, 1)
                    if s == 1 and not last:
                        xnT_rest(t + 1)
                    top_two(n)
                    if s == 0 and not first:
                        add_down(16 * t, SETS * t)
                    if s == 0 and not last:
                        stats3(t + 1)
                    dve.wait_ge(u3_hi, n + 1)
                    dve.tensor_tensor(u3l[:], hh[:], u3h[:].bitcast(F32), ALU.subtract).then_inc(u3_lo, 1)
                    if s == 0 and not last:
                        norm3(t + 1)

            for half in range(HALVES):
                t0, n0 = half * TILES, ENDS[1 + half]
                if half == 0:
                    dve.wait_ge(y_out, 16 * TILES)
                stats3(t0)
                norm3(t0)
                for n in range(n0, n0 + 4):
                    split_piece(dve, n, False)
                xnT_rest(t0)
                for n in range(n0 + 4, n0 + NP3):
                    split_piece(dve, n, False)
                tile3(t0, True, False)
                with dve.Fori(t0 + 1, t0 + TILES - 1) as t:
                    tile3(t, False, False)
                tile3(t0 + TILES - 1, False, True)
                add_down(16 * (t0 + TILES), SETS * (t0 + TILES))

        @block.tensor
        def _(pe):
            def hT_turn(t):
                pe.wait_ge(h_ok, t + 1)
                for k in range(KC):
                    ins = pe.transpose(ps[:, 7, k * P:k * P + P], h[:, k * P:k * P + P], ident)
                ins.then_inc(hT_ps, 1)

            def project(bank, piece, wide, col, weights=False):
                for k in range(KC):
                    at = piece + (k // 2 if wide == 512 else k)
                    lo = (k % 2) * 512 if wide == 512 else col
                    if weights:
                        pe.wait_ge(w_lo, at + 1)
                    ins = mm3(pe, ps[:, bank], hTh[:, k], hTl[:, k], W1h[:, at, lo:lo + 512],
                              W1l[:, at, lo:lo + 512], k == 0, k == KC - 1)
                return ins

            def onT_turn():
                for j in range(H):
                    ins = pe.transpose(ps[:, 4 + j // 4, (j % 4) * P:(j % 4) * P + P], sc[:, j], ident)
                    if j % 4 == 3:
                        ins.then_inc(onT_ps, 1)

            def out_project():
                for j in range(H):
                    at, lo = O0 + j // 2, (j % 2) * 512
                    ins = mm3(pe, ps[:, 6], onTh[:, j], onTl[:, j], W1h[:, at, lo:lo + 512],
                              W1l[:, at, lo:lo + 512], j == 0, j == H - 1)
                ins.then_inc(attn_ps, 1)

            def step(t, first, last):
                pe.wait_ge(hT_lo, t + 1)
                project(0, Q0, 512, 0, first)
                project(1, K0, 512, 0, first).then_inc(qk_ps, 1)
                if not first:
                    pe.wait_ge(on_ok, t)
                    onT_turn()
                for j in range(2):
                    ins = project(2 + j, V0, 1024, 512 * j, first)
                ins.then_inc(v_ps, 1)
                if not first:
                    pe.wait_ge(onT_lo, 2 * t)
                    pe.wait_ge(state_sum, t)
                    out_project()
                pe.wait_ge(qk_ok, t + 1)
                qkv = qk[:].rearrange("p h d -> p (h d)")
                for j in range(2 * PAIRS):
                    ins = pe.transpose(ps[:, j // PAIRS, (j % PAIRS) * P:(j % PAIRS) * P + P],
                                       qkv[:, j * P:j * P + P], ident)
                    if j % PAIRS == PAIRS - 1:
                        ins.then_inc(qkT_ps, 1)
                project(4, G0, 1024, 0, first).then_inc(g_ps, 1)
                pe.wait_ge(kT_ok, t + 1)
                pe.wait_ge(qT_ok, 2 * t + 2)
                for r in range(PAIRS):
                    ins = pe.matmul(ps[:, r // 2, (r % 2) * 256:(r % 2) * 256 + 256], kT[:, r],
                                    qbd[:, r].rearrange("p a i -> p (a i)"), start=True, stop=True)
                ins.then_inc(s_ps, 1)
                project(5, G0, 1024, 512, first).then_inc(g_ps, 1)
                if not last:
                    hT_turn(t + 1)
                pe.wait_ge(s_ok, t + 1)
                pe.wait_ge(v_ok, t + 1)
                pe.wait_ge(state_ok, t + 1)
                b = t % B
                for j in range(H):
                    o = ps[:, 2 + j // 4, (j % 4) * DV:(j % 4) * DV + DV]
                    if isinstance(t, int):
                        s_in = state[:, b, (j // 2) * DV:(j // 2) * DV + DV]
                    else:
                        s_in = state[:, bass.ds(b, 1), (j // 2) * DV:(j // 2) * DV + DV].rearrange("p a n -> p (a n)")
                    pe.matmul(o, sc[:, j], v[:, j], start=True, stop=False)
                    ins = pe.matmul(o, qbd[:, j // 2, j % 2], s_in, start=False, stop=True)
                ins.then_inc(o_ps, 1)
                if not first:
                    pe.wait_ge(x2_ok, t)
                for j in range(H):
                    ins = pe.matmul(ps[64 * (j % 2):64 * (j % 2) + 64, 6, (j // 2) * DV:(j // 2) * DV + DV],
                                    qk[:, H + j], v[:, j], start=True, stop=True)
                ins.then_inc(u_ps, 1)

            pe.wait_ge(consts_in, 80)
            hT_turn(0)
            step(0, True, False)
            pe.wait_ge(w_lo, NP1)
            with pe.Fori(1, STEPS - 1) as t:
                step(t, False, False)
            step(STEPS - 1, False, True)
            pe.wait_ge(on_ok, STEPS)
            onT_turn()
            pe.wait_ge(onT_lo, 2 * STEPS)
            pe.wait_ge(state_sum, STEPS)
            out_project()

            def h2T_turn(k, bank):
                for s in range(SUB):
                    ins = pe.transpose(ps[:, bank, s * P:s * P + P], h2[:, s, k * P:k * P + P], ident)
                ins.then_inc(h2T_ps, 1)

            def up2(t, f, weights):
                if weights:
                    pe.wait_ge(w_lo, NP1 + f + 1)
                if f >= 2:
                    pe.wait_ge(u2_ok, FT * t + f - 1)
                for g in range(2):
                    for k in range(KC):
                        lo = 512 * g + P * k
                        ins = mm3(pe, ps[:, 4 + 2 * (f % 2) + g], W2h[:, f, lo:lo + P], W2l[:, f, lo:lo + P],
                                  h2Th[:, k], h2Tl[:, k], k == 0, k == KC - 1)
                ins.then_inc(up2_ps, 1)

            def down2_add(t, f):
                pe.wait_ge(u2_lo, FT * t + f + 1)
                if f == 0 and (not isinstance(t, int) or t > 0):
                    pe.wait_ge(y_ok, SUB * t)
                for s in range(SUB):
                    ins = mm3(pe, ps[:, s], u2h[:, f % 2, s * P:s * P + P], u2l[:, f % 2, s * P:s * P + P],
                              W2h[:, f, 1024:1536], W2l[:, f, 1024:1536], f == 0, f == FT - 1)
                ins.then_inc(down2, 1)

            def tile2(t, first, last):
                pe.wait_ge(h2T_lo, KC * t + KC)
                for f in range(FT):
                    up2(t, f, first)
                    if f == FT - 1 and not last:
                        pe.wait_ge(h2_ok, SUB * t + 2 * SUB)
                        pe.wait_ge(u2_ok, FT * t + FT - 1)
                        h2T_turn(0, 6)
                        h2T_turn(1, 7)
                    if f:
                        down2_add(t, f - 1)
                if not last:
                    pe.wait_ge(u2_ok, FT * t + FT)
                    h2T_turn(2, 4)
                    h2T_turn(3, 5)
                down2_add(t, FT - 1)

            pe.wait_ge(h2_ok, SUB)
            for k, bank in enumerate((6, 7, 4, 5)):
                h2T_turn(k, bank)
            tile2(0, True, False)
            with pe.Fori(1, TILES - 1) as t:
                tile2(t, False, False)
            tile2(TILES - 1, False, True)

            def xnT_turn(k):
                for s in range(SUB):
                    ins = pe.transpose(ps[:, 4 + k, s * P:s * P + P], xn[:, s, k * P:k * P + P], ident)
                ins.then_inc(xnT_ps, 1)

            def up3(t, s, m, weights):
                n = 4 * (SETS * t + s) + m
                if s or m >= 2:
                    pe.wait_ge(hh_ok, n - 1)
                for g in range(2):
                    for k in range(KC):
                        at, lo = 4 * s + 2 * g + k // 2, 512 * (k % 2) + P * m
                        if weights and m == 0:
                            pe.wait_ge(w_lo, weights + at + 1)
                        ins = mm3(pe, ps[:, 4 + 2 * (m % 2) + g], W3h[:, at, lo:lo + P], W3l[:, at, lo:lo + P],
                                  xnTh[:, k], xnTl[:, k], k == 0, k == KC - 1)
                ins.then_inc(up3_ps, 1)

            def down3_add(s, members, done):
                for m in members:
                    for j in range(SUB):
                        at, lo = 4 * SETS + 2 * s + m // 2, 512 * (m % 2)
                        ins = mm3(pe, ps[:, j], u3h[:, m, j * P:j * P + P], u3l[:, m, j * P:j * P + P],
                                  W3h[:, at, lo:lo + 512], W3l[:, at, lo:lo + 512],
                                  s == 0 and m == 0, s == SETS - 1 and m == 3)
                if done:
                    ins.then_inc(down3, 1)

            def tile3(t, first, last, weights=0):
                pe.wait_ge(xnT_lo, KC * t + KC)
                for m in range(4):
                    up3(t, 0, m, weights)
                if not first:
                    pe.wait_ge(u3_lo, SETS * t)
                    down3_add(1, range(4), True)
                for m in range(4):
                    up3(t, 1, m, weights)
                if weights:
                    pe.wait_ge(w_lo, weights + NP3)
                if not last:
                    pe.wait_ge(xn_ok, SUB * t + 2 * SUB)
                    pe.wait_ge(hh_ok, 4 * SETS * t + 4 * SETS - 1)
                    xnT_turn(0)
                    xnT_turn(1)
                pe.wait_ge(u3_lo, SETS * t + 1)
                if not (isinstance(t, int) and t == 0):
                    pe.wait_ge(acc_ok, SUB * t)
                down3_add(0, range(0, 2), False)
                if not last:
                    pe.wait_ge(hh_ok, 4 * SETS * t + 4 * SETS)
                    xnT_turn(2)
                    xnT_turn(3)
                down3_add(0, range(2, 4), True)

            for half in range(HALVES):
                t0, n0 = half * TILES, ENDS[1 + half]
                pe.wait_ge(xn_ok, SUB * (t0 + 1))
                for k in range(KC):
                    xnT_turn(k)
                tile3(t0, True, False, n0)
                with pe.Fori(t0 + 1, t0 + TILES - 1) as t:
                    tile3(t, False, False)
                tile3(t0 + TILES - 1, False, True)
                pe.wait_ge(u3_lo, SETS * (t0 + TILES))
                down3_add(1, range(4), True)


_INS = ["hidden_states", "attn_norm_w", "q_w", "k_w", "v_w", "g_w", "o_w", "gnorm_w", "mlp_norm_w",
        "gate_w", "down_w"]
_FFN = ["w_gate", "w_up", "w_down"]


def _constants():
    import numpy as np

    f = np.float32
    inv = (f(1.0) / np.power(f(10000.0), np.arange(0, DK, 2, dtype=f) / f(DK))).astype(f)
    ang = (np.arange(L, dtype=f)[:, None] * inv).astype(f).astype(np.float64)
    cos, sin = np.cos(ang), np.sin(ang)
    by_chunk = lambda a: a.reshape(CH, P, DK).transpose(1, 0, 2).reshape(P, CH * DK)
    gamma = 1.0 - 2.0 ** (-5.0 - np.arange(H))
    i = np.arange(P)
    t = np.zeros((P, NCONST), np.float32)
    t[:, COS:COS + CH * DK] = by_chunk(np.concatenate([cos, cos], 1))
    t[:, SIN:SIN + CH * DK] = by_chunk(np.concatenate([-sin, sin], 1))
    t[:, DEC:DEC + H] = gamma[None] ** (i[:, None] + 1.0) * DK ** -0.5
    t[:, DEC + H:DEC + 2 * H] = gamma[None] ** -(i[:, None] + 1.0)
    for r in range(PAIRS):
        for a in range(2):
            t[64 * a:64 * a + 64, GAM + r * DV:GAM + (r + 1) * DV] = gamma[2 * r + a] ** P
    t[:, MASK:MASK + P] = i[:, None] <= i[None, :]
    t[:, IDN:IDN + P] = np.eye(P)
    return t


def kernel(**inputs):
    import numpy as _np
    import concourse.bacc as _bacc
    from concourse import mybir as _mybir
    from concourse.bass_utils import run_bass_kernel_spmd as _run

    nc = _bacc.Bacc("TRN2", target_bir_lowering=False, num_devices=1)
    arrays, args = {}, []
    named = [("L0_attn_" + n) for n in _INS] + [("L0_ffn_" + n) for n in _FFN]
    for name in named:
        arrays[name] = _np.ascontiguousarray(inputs[name])
    arrays["constants"] = _constants()
    for name, a in arrays.items():
        args.append(nc.dram_tensor(name, a.shape, _mybir.dt.from_np(a.dtype), kind="ExternalInput").ap())
    out = nc.dram_tensor("out_0", (B, L, D), _mybir.dt.float32, kind="ExternalOutput").ap()
    build_program(nc, *args, out)
    r = _run(nc, [arrays], core_ids=[0])
    return r.results[0]["out_0"]
```

```python
from contextlib import ExitStack

import concourse.bass as bass
from concourse import mybir

F32 = mybir.dt.float32
F32R = mybir.dt.float32r
BF16 = mybir.dt.bfloat16
ALU = mybir.AluOpType
ACT = mybir.ActivationFunctionType
AX_X = mybir.AxisListType.X

P = 128
B, L, D = 4, 1024, 512
H, DK, DV = 8, 64, 128
KC = D // P
CH = L // P
STEPS = B * CH
PAIRS = H // 2
INTER = 1408
FT = INTER // P
TOK = 512
SUB = TOK // P
TILES = B * L // TOK
HID = 2048
HALVES = 2
SETS = HID // HALVES // (4 * P)
LN_EPS, RMS_EPS = 1e-5, 1e-6

PIECE = 1024
NP1 = 16
NP2 = FT + (FT + 1) // 2
NP3 = 6 * SETS
KEPT = NP3
Q0, K0, V0, G0, O0 = 0, 2, 4, 8, 12
SLOTS = 4

COS, SIN, DEC, GAM, MASK, IDN, NCONST = 0, 512, 1024, 1040, 1552, 1680, 1808


def build_program(nc, x, attn_norm_w, q_w, k_w, v_w, g_w, o_w, gnorm_w, mlp_norm_w, gate_w, down_w,
                  f_gate_w, f_up_w, f_down_w, consts, out):
    x_rows = x.rearrange("b (c p) d -> (b c) p d", p=P)
    x_tiles = x.rearrange("b (t s p) d -> (b t) p s d", s=SUB, p=P)
    out_tiles = out.rearrange("b (t s p) d -> (b t) p s d", s=SUB, p=P)
    x2_dram = nc.dram_tensor("x2_dram", (B * L, D), F32, kind="Internal").ap()
    y_dram = nc.dram_tensor("y_dram", (B * L, D), F32, kind="Internal").ap()
    z_dram = nc.dram_tensor("z_dram", (B * L, D), F32, kind="Internal").ap()
    x2_rows = x2_dram.rearrange("(n p) d -> n p d", p=P)
    tiles_of = lambda a: a.rearrange("(t s p) d -> t p s d", s=SUB, p=P)
    x2_tiles, y_tiles, z_tiles = tiles_of(x2_dram), tiles_of(y_dram), tiles_of(z_dram)

    with ExitStack() as ctx:
        def sem(name):
            return ctx.enter_context(nc.semaphore(name))

        def sb(stack, name, shape, dt=F32):
            return stack.enter_context(nc.sbuf_tensor(name, shape, dt))

        ps = ctx.enter_context(nc.psum_tensor("ps", [P, 8, 512], F32))

        stage = sb(ctx, "stage", [P, SLOTS, PIECE])
        idn = sb(ctx, "idn", [P, P])
        norms = sb(ctx, "norms", [P, 2 * KC + 1])
        ssq = sb(ctx, "ssq", [P, SUB])
        sme = sb(ctx, "sme", [P, SUB])
        srs = sb(ctx, "srs", [P, SUB])
        st3 = sb(ctx, "st3", [P, SUB, 6])
        mv3 = sb(ctx, "mv3", [P, SUB, 2])
        ve3 = sb(ctx, "ve3", [P, SUB])
        rs3 = sb(ctx, "rs3", [P, SUB])
        pool_c = sb(ctx, "pool_c", [P, 3, 8])
        ident = idn[:]

        Wh = sb(ctx, "Wh", [P, KEPT, PIECE], F32R)
        Wl = sb(ctx, "Wl", [P, KEPT, PIECE], F32R)

        with ExitStack() as c1:
            tab = sb(c1, "tab", [P, IDN])
            hTh = sb(c1, "hTh", [P, KC, P], F32R)
            hTl = sb(c1, "hTl", [P, KC, P], F32R)
            xt = sb(c1, "xt", [P, D])
            qk = sb(c1, "qk", [P, 2 * H, DK])
            state = sb(c1, "state", [P, B, PAIRS * DV])
            qbd = sb(c1, "qbd", [P, PAIRS, 2, P])
            v = sb(c1, "v", [P, H, DV])
            sg = sb(c1, "sg", [P, H, DV])
            sc = sb(c1, "sc", [P, H, P])
            rs = sb(c1, "rs", [P, 2 * H, DK])
            rc = sb(c1, "rc", [P, 2 * H, DK])
            x1 = sb(c1, "x1", [P, 2, D])
            onTh = sb(c1, "onTh", [P, H, P], F32R)
            onTl = sb(c1, "onTl", [P, H, P], F32R)
            W1h = sb(c1, "W1h", [P, NP1 - KEPT, PIECE], F32R)
            W1l = sb(c1, "W1l", [P, NP1 - KEPT, PIECE], F32R)
            st = sb(c1, "st", [P, 6])
            mv = sb(c1, "mv", [P, 2])
            nrm = sb(c1, "nrm", [P, 6])
            oss = sb(c1, "oss", [P, H])
            ome = sb(c1, "ome", [P, H])
            ors = sb(c1, "ors", [P, H])
            rc_flat, rs_flat = (a[:].rearrange("p h d -> p (h d)") for a in (rc, rs))
            kT = rc_flat[:, 0:PAIRS * P].rearrange("p (r j) -> p r j", r=PAIRS)
            x2 = rc_flat[:, PAIRS * P:PAIRS * P + D]
            h = rs_flat[:, 0:D]

        x2t = sb(ctx, "x2t", [P, SUB, D])
        h2 = sb(ctx, "h2", [P, SUB, D])
        res = sb(ctx, "res", [P, SUB, D])
        h2Th = sb(ctx, "h2Th", [P, KC, TOK], F32R)
        h2Tl = sb(ctx, "h2Tl", [P, KC, TOK], F32R)
        sg2 = sb(ctx, "sg2", [P, 2, TOK])
        with ExitStack() as c2:
            W2h = sb(c2, "W2h", [P, 2 * (NP2 - KEPT) - FT % 2, PIECE // 2], F32R)
            W2l = sb(c2, "W2l", [P, 2 * (NP2 - KEPT) - FT % 2, PIECE // 2], F32R)
            u2 = sb(c2, "u2", [P, 2, TOK])
            u2h = sb(c2, "u2h", [P, 2, TOK], F32R)
            u2l = sb(c2, "u2l", [P, 2, TOK], F32R)
        with ExitStack() as c3:
            hh = sb(c3, "hh", [P, 4, TOK])
            ab = sb(c3, "ab", [P, 4, TOK])
            cmp = sb(c3, "cmp", [P, 6, TOK], BF16)
            win = sb(c3, "win", [P, 4, TOK], BF16)
            u3h = sb(c3, "u3h", [P, 4, TOK], F32R)
            u3l = sb(c3, "u3l", [P, 4, TOK], F32R)

        consts_in = sem("consts_in")
        pool_c_set = sem("pool_c_set")
        staged = [sem(f"staged{i}") for i in range(SLOTS)]
        w_hi = sem("w_hi")
        w_lo = sem("w_lo")
        x_in = sem("x_in")
        stat = sem("stat")
        mean_var = sem("mean_var")
        nrm_chain = sem("nrm_chain")
        rstd_ok = sem("rstd_ok")
        x1_ok = sem("x1_ok")
        h_ok = sem("h_ok")
        hT_ps = sem("hT_ps")
        hT_hi = sem("hT_hi")
        hT_lo = sem("hT_lo")
        qk_ps = sem("qk_ps")
        rope_prod = sem("rope_prod")
        rope_sum = sem("rope_sum")
        qk_ok = sem("qk_ok")
        qkT_ps = sem("qkT_ps")
        kT_ok = sem("kT_ok")
        qT_ok = sem("qT_ok")
        qbd_zero = sem("qbd_zero")
        v_ps = sem("v_ps")
        v_ok = sem("v_ok")
        g_ps = sem("g_ps")
        sg_ok = sem("sg_ok")
        s_ps = sem("s_ps")
        s_ok = sem("s_ok")
        o_ps = sem("o_ps")
        osq_ok = sem("osq_ok")
        oss_ok = sem("oss_ok")
        ome_ok = sem("ome_ok")
        ors_ok = sem("ors_ok")
        og_ok = sem("og_ok")
        on_ok = sem("on_ok")
        onT_ps = sem("onT_ps")
        onT_hi = sem("onT_hi")
        onT_lo = sem("onT_lo")
        attn_ps = sem("attn_ps")
        x2_ok = sem("x2_ok")
        x2_out = sem("x2_out")
        u_ps = sem("u_ps")
        state_sum = sem("state_sum")
        state_ok = sem("state_ok")
        x2t_in = sem("x2t_in")
        xres_in = sem("xres_in")
        res_ok = sem("res_ok")
        ssq_ok = sem("ssq_ok")
        sme_ok = sem("sme_ok")
        srs_ok = sem("srs_ok")
        h2_ok = sem("h2_ok")
        h2T_ps = sem("h2T_ps")
        h2T_hi = sem("h2T_hi")
        h2T_lo = sem("h2T_lo")
        up2_ps = sem("up2_ps")
        sg2_ok = sem("sg2_ok")
        u2_ok = sem("u2_ok")
        u2_hi = sem("u2_hi")
        u2_lo = sem("u2_lo")
        down2 = sem("down2")
        y_ok = sem("y_ok")
        y_out = sem("y_out")
        yt_in = sem("yt_in")
        st3_ok = sem("st3_ok")
        mv3_ok = sem("mv3_ok")
        ve3_ok = sem("ve3_ok")
        rs3_ok = sem("rs3_ok")
        xn_ok = sem("xn_ok")
        xnT_ps = sem("xnT_ps")
        xnT_hi = sem("xnT_hi")
        xnT_lo = sem("xnT_lo")
        up3_ps = sem("up3_ps")
        sg3_ok = sem("sg3_ok")
        hh_ok = sem("hh_ok")
        ab_ok = sem("ab_ok")
        cmp_ok = sem("cmp_ok")
        win_ok = sem("win_ok")
        win2_ok = sem("win2_ok")
        kept = sem("kept")
        u3_hi = sem("u3_hi")
        u3_lo = sem("u3_lo")
        down3 = sem("down3")
        acc_in = sem("acc_in")
        acc_ok = sem("acc_ok")
        acc_out = sem("acc_out")

        def place(phase, at, lo, width):
            if at < KEPT:
                return Wh[:, at, lo:lo + width], Wl[:, at, lo:lo + width]
            two = (W1h, W1l) if phase == 1 else (W2h, W2l)
            if phase == 1:
                return tuple(w[:, at - KEPT, lo:lo + width] for w in two)
            half, lo = 2 * (at - KEPT) + lo // 512, lo % 512
            if width <= 512:
                return tuple(w[:, half, lo:lo + width] for w in two)
            return tuple(w[:, half:half + 2].rearrange("p a n -> p (a n)") for w in two)

        def rows2(w, j, cols=slice(None)):
            return w.rearrange("(a p) n -> p a n", p=P)[:, 2 * j:2 * j + 2, cols]

        def pieces():
            for w, first in ((q_w, Q0), (k_w, K0)):
                for j in range(2):
                    yield [(0, rows2(w, j))], [(512 * a, 512, 2 * j + a) for a in range(2)], 1, first + j
            for w, first in ((v_w, V0), (g_w, G0)):
                for kc in range(KC):
                    yield ([(0, w.rearrange("(a p) n -> p a n", p=P)[:, kc:kc + 1, :])],
                           [(0, 1024, kc)], 1, first + kc)
            for j in range(4):
                yield [(0, rows2(o_w, j))], [(0, 1024, 2 * KC)], 1, O0 + j
            gate = gate_w.rearrange("(a p) n -> p a n", p=P)
            down = down_w.rearrange("(f p) n -> p f n", p=P)
            for f in range(FT):
                yield ([(512 * g, gate[:, :, g * INTER + f * P:g * INTER + f * P + P]) for g in range(2)],
                       [(P * kc, P, KC + kc) for kc in range(KC)], 2, f)
                if f % 2 or f == FT - 1:
                    n = f % 2 + 1
                    yield [(0, down[:, f + 1 - n:f + 1, :])], [(0, 512 * n, None)], 2, FT + f // 2
            fdown = f_down_w.rearrange("(g p r) n -> g p r n", p=P, r=4)
            for half in range(HALVES):
                for s in range(SETS):
                    c0 = (half * SETS + s) * 512
                    for w, k in ((f_gate_w, 0), (f_up_w, 2)):
                        for j in range(2):
                            yield [(0, rows2(w, j, slice(c0, c0 + 512)))], "group", 3, 4 * s + k + j
                for s in range(SETS):
                    for j in range(2):
                        yield ([(0, fdown[half * SETS + s][:, 2 * j:2 * j + 2, :])],
                               [(0, 1024, None)], 3, 4 * SETS + 2 * s + j)

        PIECES = list(pieces())
        ENDS = [NP1, NP1 + NP2, NP1 + NP2 + NP3, NP1 + NP2 + 2 * NP3]
        assert len(PIECES) == ENDS[-1]
        loads_before = [sum(len(PIECES[m][0]) for m in range(n + 1) if m % SLOTS == n % SLOTS)
                        for n in range(len(PIECES))]

        def need(eng, s, n):
            if not isinstance(n, int) or n > 0:
                eng.wait_ge(s, n)

        def load_pieces(eng, first, end):
            for n in range(first, end):
                need(eng, w_lo, n - SLOTS + 1)
                for col, src in PIECES[n][0]:
                    width = src.shape[1] * src.shape[2]
                    dst = stage[:, n % SLOTS, col:col + width].rearrange("p (a n) -> p a n", a=src.shape[1])
                    eng.dma_start(dst, src).then_inc(staged[n % SLOTS], 16)

        def split_pieces(eng, first, end, hi):
            for n in range(first, end):
                loads, parts, phase, at = PIECES[n]
                raw = stage[:, n % SLOTS]
                eng.wait_ge(staged[n % SLOTS], 16 * loads_before[n])
                if not hi:
                    eng.wait_ge(w_hi, n + 1)
                if parts == "group":
                    for a in range(2):
                        src = raw[:, 512 * a:512 * a + 512].rearrange("p (g r) -> p r g", r=4)
                        dh, dl = (w.rearrange("p (r g) -> p r g", r=4) for w in place(phase, at, 512 * a, 512))
                        if hi:
                            ins = eng.copy(dh, src)
                        else:
                            ins = eng.tensor_tensor(dl, src, dh.bitcast(F32), ALU.subtract)
                else:
                    for col, width, norm in parts:
                        scale = norms[:, norm:norm + 1] if norm is not None else 1.0
                        src = raw[:, col:col + width]
                        dh, dl = place(phase, at, col, width)
                        if phase == 2 and at < FT:
                            src = raw.rearrange("p (g n) -> p g n", g=2)[:, :, col:col + width]
                            dh, dl = (w.rearrange("p (g n) -> p g n", g=2)[:, :, col:col + width]
                                      for w in place(phase, at, 0, PIECE))
                        if hi:
                            ins = eng.activation(dh, src, ACT.Copy, scale=scale)
                        else:
                            ins = eng.scalar_tensor_tensor(out=dl, in0=src, scalar=scale, in1=dh.bitcast(F32),
                                                           op0=ALU.mult, op1=ALU.subtract)
                ins.then_inc(w_hi if hi else w_lo, 1)

        def mm3(pe, dst, lh, ll, rh, rl, start, stop):
            pe.matmul(dst, lh, rh, start=start, stop=False)
            pe.matmul(dst, lh, rl, start=False, stop=False)
            return pe.matmul(dst, ll, rh, start=False, stop=stop)

        def row_tile(t):
            return (t % B) * CH + t // B

        def due2(f):
            upto = lambda f: min(NP2, 3 * (f + 2) // 2 + 3)
            return NP1 + (upto(f - 1) if f else 4), NP1 + max(upto(f), 4)

        def h2T_banks(t):
            return (7, 4, 5, 6) if isinstance(t, int) and t == 0 else (6, 7, 4, 5)

        t1 = TILES
        NEW = range(ENDS[2], ENDS[3])
        SCHEDULE3 = [((0,), dict(first=True)), ((1, t1 - 1), {}),
                     ((t1 - 1,), dict(fresh=[(), (), (), ()] + list(NEW[0:4]))),
                     ((t1,), dict(fresh=list(NEW[4:8]) + [(), (), (), ()] + list(NEW[8:12]))),
                     ((t1 + 1, 2 * t1 - 1), {}), ((2 * t1 - 1,), dict(last=True))]

        def run3(eng, tile, turns, how):
            if len(turns) == 1:
                tile(turns[0], **how)
            else:
                with eng.Fori(*turns) as t:
                    tile(t, **how)

        def tile_at(a, i):
            return a[bass.ds(i, 1)].rearrange("a p s d -> p (a s) d")

        block = ctx.enter_context(nc.Block())

        @block.sync
        def _(sp):
            sp.dma_start(xt[:], x_rows[row_tile(0)]).then_inc(x_in, 16)
            sp.dma_start(tab[:], consts[:, 0:IDN]).then_inc(consts_in, 16)
            sp.dma_start(idn[:], consts[:, IDN:IDN + P]).then_inc(consts_in, 16)
            sp.dma_start(norms[:, 0:KC], attn_norm_w.rearrange("(k p) -> p k", p=P), allow_slow_non_contiguous=True).then_inc(consts_in, 16)
            sp.dma_start(norms[:, KC:2 * KC], mlp_norm_w.rearrange("(k p) -> p k", p=P), allow_slow_non_contiguous=True).then_inc(consts_in, 16)
            sp.dma_start(norms[:, 2 * KC:2 * KC + 1], gnorm_w.rearrange("(p k) -> p k", k=1), allow_slow_non_contiguous=True).then_inc(consts_in, 16)
            load_pieces(sp, 0, 4)
            sp.wait_ge(x1_ok, 1)
            sp.dma_start(xt[:], x_rows[row_tile(1)]).then_inc(x_in, 16)
            load_pieces(sp, 4, 12)
            sp.wait_ge(x1_ok, 2)
            sp.dma_start(xt[:], x_rows[row_tile(2)]).then_inc(x_in, 16)
            load_pieces(sp, 12, NP1)

            def row_at(a, t):
                return a[bass.ds(row_tile(t), 1)].rearrange("a p d -> p (a d)")

            def load_x(t):
                sp.wait_ge(x1_ok, t)
                sp.dma_start(xt[:], row_at(x_rows, t)).then_inc(x_in, 16)

            def store_x2(t):
                sp.wait_ge(x2_ok, t + 1)
                sp.dma_start(row_at(x2_rows, t), x2).then_inc(x2_out, 16)

            with sp.Fori(0, STEPS - 3) as t:
                store_x2(t)
                load_x(t + 3)
            load_pieces(sp, NP1, NP1 + SLOTS)
            for t in range(STEPS - 3, STEPS - 1):
                sp.wait_ge(x2_ok, t + 1)
                sp.dma_start(x2_rows[row_tile(t)], x2).then_inc(x2_out, 16)

            sp.wait_ge(o_ps, STEPS)
            sp.dma_start(x2t[:], x2_tiles[0]).then_inc(x2t_in, 16)
            sp.dma_start(res[:], x_tiles[0]).then_inc(xres_in, 16)
            sp.wait_ge(x2_ok, STEPS)
            sp.dma_start(x2_rows[row_tile(STEPS - 1)], x2).then_inc(x2_out, 16)
            load_pieces(sp, NP1 + SLOTS, NP1 + 9)
            sp.wait_ge(res_ok, 1)
            sp.wait_ge(x2_out, 16 * STEPS)
            sp.dma_start(x2t[:], x2_tiles[1]).then_inc(x2t_in, 16)
            load_pieces(sp, NP1 + 9, ENDS[1])
            with sp.Fori(3, TILES + 1) as i:
                sp.wait_ge(y_ok, SUB * (i - 2))
                sp.dma_start(tile_at(y_tiles, i - 3), res[:]).then_inc(y_out, 16)
                sp.wait_ge(y_out, 16 * (i - 2))
                sp.dma_start(res[:], tile_at(x_tiles, i - 2)).then_inc(xres_in, 16)
                sp.wait_ge(res_ok, i - 1)
                sp.dma_start(x2t[:], tile_at(x2_tiles, i - 1)).then_inc(x2t_in, 16)
            t = TILES - 2
            sp.wait_ge(y_ok, SUB * (t + 1))
            sp.dma_start(y_tiles[t], res[:]).then_inc(y_out, 16)
            sp.wait_ge(y_out, 16 * (t + 1))
            sp.dma_start(res[:], x_tiles[t + 1]).then_inc(xres_in, 16)

            load_pieces(sp, ENDS[1], ENDS[1] + SLOTS)
            sp.wait_ge(res_ok, TILES)
            sp.dma_start(x2t[:], y_tiles[0]).then_inc(yt_in, 16)
            load_pieces(sp, ENDS[1] + SLOTS, ENDS[2])
            sp.wait_ge(y_ok, SUB * TILES)
            sp.dma_start(y_tiles[TILES - 1], res[:]).then_inc(y_out, 16)
            sp.wait_ge(y_out, 16 * TILES)
            sp.dma_start(res[:], y_tiles[0]).then_inc(acc_in, 16)
            sp.wait_ge(xn_ok, SUB)
            sp.dma_start(x2t[:], y_tiles[1]).then_inc(yt_in, 16)

            def fetch_y(t):
                sp.wait_ge(xn_ok, SUB * t)
                sp.dma_start(x2t[:], y_tiles[t % TILES]).then_inc(yt_in, 16)

            def store_sum(t):
                src, dst = (y_tiles, z_tiles) if t < TILES else (z_tiles, out_tiles)
                sp.wait_ge(acc_ok, SUB * (t + 1))
                sp.dma_start(dst[t % TILES], res[:]).then_inc(acc_out, 16)
                sp.wait_ge(acc_out, 16 * (t + 1))
                if t < HALVES * TILES - 1:
                    src = y_tiles if t + 1 < TILES else z_tiles
                    sp.dma_start(res[:], src[(t + 1) % TILES]).then_inc(acc_in, 16)

            for half in range(HALVES):
                t0 = half * TILES
                src, dst = (y_tiles, z_tiles) if half == 0 else (z_tiles, out_tiles)
                with sp.Fori(3, TILES + 1) as i:
                    sp.wait_ge(xn_ok, SUB * (i - 1 + t0))
                    sp.dma_start(x2t[:], tile_at(y_tiles, i - 1)).then_inc(yt_in, 16)
                    sp.wait_ge(acc_ok, SUB * (i - 2 + t0))
                    sp.dma_start(tile_at(dst, i - 3), res[:]).then_inc(acc_out, 16)
                    sp.wait_ge(acc_out, 16 * (i - 2 + t0))
                    sp.dma_start(res[:], tile_at(src, i - 2)).then_inc(acc_in, 16)
                if half == 0:
                    fetch_y(TILES)
                    load_pieces(sp, ENDS[2], ENDS[2] + SLOTS)
                    store_sum(TILES - 2)
                    fetch_y(TILES + 1)
                    load_pieces(sp, ENDS[2] + SLOTS, ENDS[3])
                    store_sum(TILES - 1)
                else:
                    store_sum(2 * TILES - 2)
                    store_sum(2 * TILES - 1)

        @block.gpsimd
        def _(pool):
            for at, value in enumerate((-0.5, LN_EPS, RMS_EPS)):
                pool.memset(pool_c[:, at], value).then_inc(pool_c_set, 1)
            pool.memset(qbd[:], 0.0).then_inc(qbd_zero, 1)
            pool.wait_ge(pool_c_set, 3)
            minus_half, ln_eps, rms_eps = (pool_c[:, at] for at in range(3))

            def norm_scalars(t):
                var, ve, rstd, vr, vrr, vrre, r2 = mv[:, 1:2], *(nrm[:, i:i + 1] for i in range(6))
                pool.wait_ge(mean_var, t + 1)
                need(pool, h_ok, t)
                pool.tensor_tensor(ve, var, ln_eps[:, 0:1], ALU.add).then_inc(nrm_chain, 1)
                pool.wait_ge(nrm_chain, 4 * t + 1)
                pool.tensor_tensor(rstd, ve, minus_half[:, 0:1], ALU.pow).then_inc(rstd_ok, 1)
                pool.wait_ge(rstd_ok, 2 * t + 1)
                pool.tensor_tensor(vr, var, rstd, ALU.mult).then_inc(nrm_chain, 1)
                pool.wait_ge(nrm_chain, 4 * t + 2)
                pool.tensor_tensor(vrr, vr, rstd, ALU.mult).then_inc(nrm_chain, 1)
                pool.wait_ge(nrm_chain, 4 * t + 3)
                pool.tensor_tensor(vrre, vrr, rms_eps[:, 0:1], ALU.add).then_inc(nrm_chain, 1)
                pool.wait_ge(nrm_chain, 4 * t + 4)
                pool.tensor_tensor(r2, vrre, minus_half[:, 0:1], ALU.pow).then_inc(rstd_ok, 1)

            def head_scalars(t):
                pool.wait_ge(oss_ok, t + 1)
                pool.tensor_tensor(ome[:], oss[:], rms_eps, ALU.add).then_inc(ome_ok, 1)
                pool.wait_ge(ome_ok, t + 1)
                pool.tensor_tensor(ors[:], ome[:], minus_half, ALU.pow).then_inc(ors_ok, 1)

            norm_scalars(0)
            norm_scalars(1)
            head_scalars(0)
            with pool.Fori(1, STEPS - 1) as t:
                norm_scalars(t + 1)
                head_scalars(t)
            head_scalars(STEPS - 1)

            def rms_scalars(t):
                pool.wait_ge(ssq_ok, SUB * t + SUB)
                pool.tensor_tensor(sme[:], ssq[:], rms_eps[:, 0:SUB], ALU.add).then_inc(sme_ok, 1)
                pool.wait_ge(sme_ok, t + 1)
                pool.tensor_tensor(srs[:], sme[:], minus_half[:, 0:SUB], ALU.pow).then_inc(srs_ok, 1)

            def residual(t):
                pool.wait_ge(xres_in, 16 * t + 16)
                pool.wait_ge(x2t_in, 16 * t + 16)
                pool.wait_ge(h2_ok, SUB * t + SUB)
                pool.tensor_tensor(res[:], res[:], x2t[:], ALU.add).then_inc(res_ok, 1)

            rms_scalars(0)
            residual(0)
            with pool.Fori(1, TILES) as t:
                rms_scalars(t)
                residual(t)

            with pool.Fori(0, HALVES * TILES) as t:
                pool.wait_ge(mv3_ok, SUB * t + SUB)
                pool.tensor_tensor(ve3[:], mv3[:, :, 1], ln_eps[:, 0:SUB], ALU.add).then_inc(ve3_ok, 1)
                pool.wait_ge(ve3_ok, t + 1)
                pool.tensor_tensor(rs3[:], ve3[:], minus_half[:, 0:SUB], ALU.pow).then_inc(rs3_ok, 1)

        @block.scalar
        def _(act):
            def make_h(t):
                act.wait_ge(x1_ok, t + 1)
                act.wait_ge(rstd_ok, 2 * t + 2)
                slot = x1[:, t % 2] if isinstance(t, int) else x1[:, bass.ds(t % 2, 1)].rearrange("p a d -> p (a d)")
                act.activation(h, slot, ACT.Copy, scale=nrm[:, 5:6]).then_inc(h_ok, 1)

            def hT_round(t):
                act.wait_ge(hT_ps, t + 1)
                act.copy(hTh[:].rearrange("p k t -> p (k t)"), ps[:, 7]).then_inc(hT_hi, 1)

            def onT_round(t):
                for j in range(2):
                    act.wait_ge(onT_ps, 2 * t + j + 1)
                    act.copy(onTh[:, 4 * j:4 * j + 4].rearrange("p h t -> p (h t)"), ps[:, 4 + j]).then_inc(onT_hi, 1)

            def step(t, first, last):
                if not first:
                    for j in range(2):
                        act.wait_ge(onT_ps, 2 * t + j - 1)
                        act.copy(onTh[:, 4 * j:4 * j + 4].rearrange("p h t -> p (h t)"), ps[:, 4 + j]).then_inc(onT_hi, 1)
                if first:
                    split_pieces(act, 8, 11, True)
                act.wait_ge(v_ps, t + 1)
                act.copy(v[:].rearrange("p h e -> p (h e)"), ps[:, 2:4].rearrange("p a n -> p (a n)")).then_inc(v_ok, 1)
                if first:
                    split_pieces(act, 11, 12, True)
                act.wait_ge(qkT_ps, 2 * t + 1)
                qT = ps[:, 0].rearrange("p (r i) -> p r i", r=PAIRS)
                if first:
                    act.wait_ge(qbd_zero, 1)
                act.copy(qbd[0:64, :, 0], qT[0:64]).then_inc(qT_ok, 1)
                act.copy(qbd[64:128, :, 1], qT[64:128]).then_inc(qT_ok, 1)
                act.wait_ge(qkT_ps, 2 * t + 2)
                act.copy(kT.rearrange("p r j -> p (r j)"), ps[:, 1]).then_inc(kT_ok, 1)
                act.wait_ge(g_ps, 2 * t + 1)
                act.activation(sg[:, 0:4].rearrange("p h e -> p (h e)"), ps[:, 4], ACT.Silu).then_inc(sg_ok, 1)
                if not last:
                    make_h(t + 1)
                if first:
                    split_pieces(act, 12, 14, True)
                act.wait_ge(g_ps, 2 * t + 2)
                act.activation(sg[:, 4:8].rearrange("p h e -> p (h e)"), ps[:, 5], ACT.Silu).then_inc(sg_ok, 1)
                if not last:
                    hT_round(t + 1)
                act.wait_ge(o_ps, t + 1)
                act.activation(rs[:].rearrange("p h e -> p (h e)"), ps[:, 2:4].rearrange("p a n -> p (a n)"),
                               ACT.Square, scale=DV ** -0.5).then_inc(osq_ok, 1)

            act.wait_ge(consts_in, 80)
            split_pieces(act, 0, 2, True)
            make_h(0)
            hT_round(0)
            split_pieces(act, 2, 8, True)
            step(0, True, False)
            split_pieces(act, 14, NP1, True)
            with act.Fori(1, STEPS - 1) as t:
                step(t, False, False)
            step(STEPS - 1, False, True)
            split_pieces(act, NP1, NP1 + 1, True)
            onT_round(STEPS - 1)

            def square_x2(t):
                act.wait_ge(x2t_in, 16 * t + 16)
                for s in range(SUB):
                    act.activation(h2[:, s], x2t[:, s], ACT.Square, scale=D ** -0.5,
                                   accum_out=ssq[:, s:s + 1]).then_inc(ssq_ok, 1)

            def make_h2(t):
                act.wait_ge(srs_ok, t + 1)
                for s in range(SUB):
                    act.activation(h2[:, s], x2t[:, s], ACT.Copy, scale=srs[:, s:s + 1]).then_inc(h2_ok, 1)

            def h2T_round(t):
                for k, bank in enumerate(h2T_banks(t)):
                    act.wait_ge(h2T_ps, KC * t + k + 1)
                    act.copy(h2Th[:, k], ps[:, bank]).then_inc(h2T_hi, 1)

            def tile2(t, first, last):
                for f in range(FT):
                    act.wait_ge(up2_ps, FT * t + f + 1)
                    act.activation(sg2[:, f % 2], ps[:, 4 + 2 * (f % 2)], ACT.Silu).then_inc(sg2_ok, 1)
                    act.wait_ge(u2_ok, FT * t + f + 1)
                    if f >= 2:
                        act.wait_ge(down2, FT * t + f - 1)
                    act.copy(u2h[:, f % 2], u2[:, f % 2]).then_inc(u2_hi, 1)
                    if first:
                        split_pieces(act, *due2(f), True)
                    if last and f:
                        split_pieces(act, ENDS[1] + f - 1, ENDS[1] + f, True)
                    if not last and f == 5:
                        square_x2(t + 1)
                    if not last and f == 6:
                        make_h2(t + 1)
                if not last:
                    h2T_round(t + 1)
                else:
                    split_pieces(act, ENDS[1] + FT - 1, ENDS[2] - 1, True)
                    h2T_round(TILES)
                    split_pieces(act, ENDS[2] - 1, ENDS[2], True)

            square_x2(0)
            make_h2(0)
            split_pieces(act, NP1 + 1, NP1 + 4, True)
            h2T_round(0)
            tile2(0, True, False)
            with act.Fori(1, TILES - 1) as t:
                tile2(t, False, False)
            tile2(TILES - 1, False, True)

            def xnT_round(t):
                for k in range(KC):
                    act.wait_ge(h2T_ps, KC * (t + TILES) + k + 1)
                    act.copy(h2Th[:, k], ps[:, 4 + k]).then_inc(h2T_hi, 1)

            def tile3(t, first=False, last=False, fresh=()):
                for s in range(SETS):
                    n = SETS * t + s
                    for m in range(4):
                        act.wait_ge(up3_ps, 4 * n + m + 1)
                        act.activation(sg2[:, m % 2], ps[:, 4 + 2 * (m % 2)], ACT.Silu).then_inc(sg3_ok, 1)
                        act.wait_ge(hh_ok, 4 * n + m + 1)
                        act.activation(ab[:, m], hh[:, m], ACT.Abs).then_inc(ab_ok, 1)
                        for piece in (p for p in fresh[4 * s + m:4 * s + m + 1] if p != ()):
                            split_pieces(act, piece, piece + 1, True)
                    if s == 1 and not last:
                        xnT_round(t + 1)
                    act.wait_ge(kept, 4 * n + 4)
                    if not (first and s == 0):
                        act.wait_ge(down3, n)
                    act.copy(u3h[:], hh[:]).then_inc(u3_hi, 1)
                    if s == 0:
                        for piece in fresh[4 * SETS:]:
                            split_pieces(act, piece, piece + 1, True)

            for step3 in SCHEDULE3:
                run3(act, tile3, *step3)

        @block.vector
        def _(dve):
            def x1_slot(t):
                return x1[:, t % 2] if isinstance(t, int) else x1[:, bass.ds(t % 2, 1)].rearrange("p a d -> p (a d)")

            def stats(t):
                dve.wait_ge(x_in, 16 * t + 16)
                dve.bn_stats(st[:, 0:6], xt[:]).then_inc(stat, 1)

            def aggregate():
                dve.bn_aggr(mv[:], st[:, 0:6]).then_inc(mean_var, 1)

            def make_x1(t):
                dve.wait_ge(rstd_ok, 2 * t + 1)
                dve.tensor_scalar(x1_slot(t), xt[:], mv[:, 0:1], nrm[:, 1:2], ALU.subtract,
                                  ALU.mult).then_inc(x1_ok, 1)

            def hT_rest(t):
                dve.wait_ge(hT_hi, t + 1)
                dve.tensor_tensor(hTl[:].rearrange("p k t -> p (k t)"), ps[:, 7],
                                  hTh[:].rearrange("p k t -> p (k t)").bitcast(F32), ALU.subtract).then_inc(hT_lo, 1)

            def onT_rest(n):
                for j in range(2):
                    dve.wait_ge(onT_hi, n - 1 + j if isinstance(n, int) else n + (j - 1))
                    dve.tensor_tensor(onTl[:, 4 * j:4 * j + 4].rearrange("p h t -> p (h t)"), ps[:, 4 + j],
                                      onTh[:, 4 * j:4 * j + 4].rearrange("p h t -> p (h t)").bitcast(F32),
                                      ALU.subtract).then_inc(onT_lo, 1)

            def add_residual(t, made):
                dve.wait_ge(qk_ok, made + 1 if made < STEPS else made)
                dve.wait_ge(attn_ps, made)
                dve.tensor_tensor(x2, x1_slot(t), ps[:, 6], ALU.add).then_inc(x2_ok, 1)

            def step(t, first, last):
                prev = t - 1 if isinstance(t, int) else None
                c = t // B
                dve.wait_ge(qk_ps, t + 1)
                qkp = ps[:, 0:2].rearrange("p a (h d) -> p (a h) d", d=DK)
                cos = tab[:, COS:COS + CH * DK].rearrange("p (c d) -> p c d", d=DK)[:, bass.ds(c, 1), :]
                sin = tab[:, SIN:SIN + CH * DK].rearrange("p (c d) -> p c d", d=DK)[:, bass.ds(c, 1), :]
                hd = DK // 2
                if not isinstance(t, int) or t > 1:
                    dve.wait_ge(x2_out, 16 * (t - 1))
                dve.tensor_tensor(rc[:], qkp, cos.broadcast_to([P, 2 * H, DK]), ALU.mult).then_inc(rope_prod, 1)
                dve.tensor_tensor(rs[:, :, 0:hd], qkp[:, :, hd:DK],
                                  sin[:, :, 0:hd].broadcast_to([P, 2 * H, hd]), ALU.mult).then_inc(rope_prod, 1)
                dve.tensor_tensor(rs[:, :, hd:DK], qkp[:, :, 0:hd],
                                  sin[:, :, hd:DK].broadcast_to([P, 2 * H, hd]), ALU.mult).then_inc(rope_prod, 1)
                if not first:
                    onT_rest(2 * t)
                dve.wait_ge(rope_prod, 3 * t + 3)
                dve.tensor_tensor(rc[:], rc[:], rs[:], ALU.add).then_inc(rope_sum, 1)
                if not last:
                    stats(t + 1)
                    dve.wait_ge(stat, t + 2)
                dve.wait_ge(rope_sum, t + 1)
                dve.tensor_tensor(qk[:], rc[:], tab[:, DEC:DEC + 2 * H].rearrange("p (h a) -> p h a", a=1)
                                  .broadcast_to([P, 2 * H, DK]), ALU.mult).then_inc(qk_ok, 1)
                if first:
                    split_pieces(dve, 8, 12, False)
                if not last:
                    aggregate()
                if not first:
                    if isinstance(t, int):
                        add_residual(t - 1, t)
                    else:
                        add_residual_prev(t)
                if not last:
                    need(dve, x2_ok, t)
                    make_x1(t + 1)
                dve.wait_ge(s_ps, t + 1)
                dve.tensor_tensor(sc[:], ps[:, 0:2].rearrange("p a (h i) -> p (a h) i", i=P),
                                  tab[:, MASK:MASK + P].rearrange("p (a i) -> p a i", a=1).broadcast_to([P, H, P]),
                                  ALU.mult).then_inc(s_ok, 1)
                if not last:
                    hT_rest(t + 1)
                if first:
                    split_pieces(dve, 12, 14, False)
                dve.wait_ge(osq_ok, t + 1)
                dve.tensor_reduce(oss[:], rs[:].rearrange("p a d -> p (a d)").rearrange("p (h e) -> p h e", e=DV),
                                  AX_X, ALU.add).then_inc(oss_ok, 1)
                dve.wait_ge(sg_ok, 2 * t + 2)
                dve.tensor_tensor(sc[:], ps[:, 2:4].rearrange("p a (h e) -> p (a h) e", e=DV), sg[:],
                                  ALU.mult).then_inc(og_ok, 1)
                if not last:
                    update_state(t)
                dve.wait_ge(ors_ok, t + 1)
                dve.wait_ge(og_ok, t + 1)
                dve.tensor_tensor(sc[:], sc[:], ors[:].rearrange("p (h a) -> p h a", a=1).broadcast_to([P, H, DV]),
                                  ALU.mult).then_inc(on_ok, 1)

            def update_state(t):
                b = t % B
                sb_ = state[:, b] if isinstance(t, int) else state[:, bass.ds(b, 1)].rearrange("p a n -> p (a n)")
                dve.wait_ge(u_ps, t + 1)
                dve.tensor_tensor(sb_, sb_, ps[:, 6], ALU.add).then_inc(state_sum, 1)
                dve.wait_ge(state_sum, t + 1)
                dve.tensor_tensor(sb_, sb_, tab[:, GAM:GAM + PAIRS * DV], ALU.mult).then_inc(state_ok, 1)

            def add_residual_prev(t):
                slot = x1[:, bass.ds((t + 1) % 2, 1)].rearrange("p a d -> p (a d)")
                dve.wait_ge(qk_ok, t + 1)
                dve.wait_ge(attn_ps, t)
                dve.tensor_tensor(x2, slot, ps[:, 6], ALU.add).then_inc(x2_ok, 1)

            dve.memset(state[:], 0.0).then_inc(state_ok, 1)
            dve.wait_ge(consts_in, 80)
            stats(0)
            dve.wait_ge(stat, 1)
            aggregate()
            make_x1(0)
            split_pieces(dve, 0, 2, False)
            hT_rest(0)
            split_pieces(dve, 2, 8, False)
            dve.wait_ge(state_ok, 1)
            step(0, True, False)
            split_pieces(dve, 14, NP1, False)
            step(1, False, False)
            with dve.Fori(2, STEPS - 1) as t:
                step(t, False, False)
            step(STEPS - 1, False, True)
            split_pieces(dve, NP1, NP1 + 1, False)
            onT_rest(2 * STEPS)
            dve.wait_ge(x2_out, 16 * (STEPS - 1))
            add_residual(STEPS - 1, STEPS)

            def stats3(t):
                dve.wait_ge(yt_in, 16 * t + 16)
                for s in range(SUB):
                    dve.bn_stats(st3[:, s], x2t[:, s]).then_inc(st3_ok, 1)
                dve.wait_ge(st3_ok, SUB * t + SUB)

            def norm3(t):
                for s in range(SUB):
                    dve.bn_aggr(mv3[:, s], st3[:, s]).then_inc(mv3_ok, 1)
                dve.wait_ge(rs3_ok, t + 1)
                for s in range(SUB):
                    dve.tensor_scalar(h2[:, s], x2t[:, s], mv3[:, s, 0:1], rs3[:, s:s + 1], ALU.subtract,
                                      ALU.mult).then_inc(xn_ok, 1)

            def h2T_rest(t):
                for k, bank in enumerate(h2T_banks(t)):
                    dve.wait_ge(h2T_hi, KC * t + k + 1)
                    dve.tensor_tensor(h2Tl[:, k], ps[:, bank], h2Th[:, k].bitcast(F32), ALU.subtract)\
                       .then_inc(h2T_lo, 1)

            def tile2(t, first, last):
                for f in range(FT):
                    dve.wait_ge(sg2_ok, FT * t + f + 1)
                    dve.tensor_tensor(u2[:, f % 2], ps[:, 5 + 2 * (f % 2)], sg2[:, f % 2], ALU.mult)\
                       .then_inc(u2_ok, 1)
                    dve.wait_ge(u2_hi, FT * t + f + 1)
                    dve.tensor_tensor(u2l[:, f % 2], u2[:, f % 2], u2h[:, f % 2].bitcast(F32), ALU.subtract)\
                       .then_inc(u2_lo, 1)
                    if first:
                        split_pieces(dve, *due2(f), False)
                    if last and f:
                        split_pieces(dve, ENDS[1] + f - 1, ENDS[1] + f, False)
                    if last and f == 5:
                        stats3(0)
                    if last and f == 6:
                        norm3(0)
                if not last:
                    h2T_rest(t + 1)
                else:
                    split_pieces(dve, ENDS[1] + FT - 1, ENDS[2] - 1, False)
                    h2T_rest(TILES)
                    split_pieces(dve, ENDS[2] - 1, ENDS[2], False)
                dve.wait_ge(down2, FT * t + FT)
                dve.wait_ge(res_ok, t + 1)
                for s in range(SUB):
                    dve.tensor_tensor(res[:, s], res[:, s], ps[:, s], ALU.add).then_inc(y_ok, 1)

            split_pieces(dve, NP1 + 1, NP1 + 4, False)
            h2T_rest(0)
            dve.wait_ge(x2_out, 16 * STEPS)
            tile2(0, True, False)
            with dve.Fori(1, TILES - 1) as t:
                tile2(t, False, False)
            tile2(TILES - 1, False, True)

            def xnT_rest(t):
                for k in range(KC):
                    dve.wait_ge(h2T_hi, KC * (t + TILES) + k + 1)
                    dve.tensor_tensor(h2Tl[:, k], ps[:, 4 + k], h2Th[:, k].bitcast(F32), ALU.subtract)\
                       .then_inc(h2T_lo, 1)

            def top_two(n):
                dve.wait_ge(ab_ok, 4 * n + 4)
                dve.tensor_tensor(cmp[:, 0:2], ab[:, 0:2], ab[:, 2:4], ALU.is_ge).then_inc(cmp_ok, 1)
                dve.tensor_tensor(cmp[:, 2], ab[:, 0], ab[:, 3], ALU.is_ge).then_inc(cmp_ok, 1)
                dve.tensor_tensor(cmp[:, 3], ab[:, 1], ab[:, 2], ALU.is_ge).then_inc(cmp_ok, 1)
                dve.tensor_tensor(cmp[:, 4], ab[:, 0], ab[:, 1], ALU.is_ge).then_inc(cmp_ok, 1)
                dve.tensor_tensor(cmp[:, 5], ab[:, 2], ab[:, 3], ALU.is_ge).then_inc(cmp_ok, 1)
                dve.wait_ge(cmp_ok, 5 * n + 5)
                dve.tensor_tensor(win[:, 0:2], cmp[:, 0:2], cmp[:, 2:4], ALU.add).then_inc(win_ok, 1)
                dve.tensor_tensor(win[:, 2], cmp[:, 0], cmp[:, 3], ALU.add).then_inc(win_ok, 1)
                dve.tensor_tensor(win[:, 3], cmp[:, 1], cmp[:, 2], ALU.add).then_inc(win_ok, 1)
                dve.wait_ge(win_ok, 3 * n + 3)
                for m, other, op in ((0, 4, ALU.add), (1, 4, ALU.subtract), (2, 5, ALU.subtract), (3, 5, ALU.add)):
                    dve.tensor_tensor(win[:, m], win[:, m], cmp[:, other], op).then_inc(win2_ok, 1)
                dve.wait_ge(win2_ok, 4 * n + 4)
                for m, op, bound in ((0, ALU.is_ge, 2.0), (1, ALU.is_ge, 1.0), (2, ALU.is_le, 0.0), (3, ALU.is_le, 1.0)):
                    dve.scalar_tensor_tensor(out=hh[:, m], in0=win[:, m], scalar=bound, in1=hh[:, m], op0=op,
                                             op1=ALU.mult).then_inc(kept, 1)

            def add_down(t, made):
                dve.wait_ge(down3, made)
                dve.wait_ge(acc_in, t)
                for s in range(SUB):
                    dve.tensor_tensor(res[:, s], res[:, s], ps[:, s], ALU.add).then_inc(acc_ok, 1)

            def tile3(t, first=False, last=False, fresh=()):
                for s in range(SETS):
                    n = SETS * t + s
                    need(dve, u3_lo, n)
                    for m in range(4):
                        dve.wait_ge(sg3_ok, 4 * n + m + 1)
                        dve.tensor_tensor(hh[:, m], ps[:, 5 + 2 * (m % 2)], sg2[:, m % 2], ALU.mult)\
                           .then_inc(hh_ok, 1)
                        for piece in (p for p in fresh[4 * s + m:4 * s + m + 1] if p != ()):
                            split_pieces(dve, piece, piece + 1, False)
                    if s == 1 and not last:
                        xnT_rest(t + 1)
                    top_two(n)
                    if s == 0 and not first:
                        add_down(16 * t, SETS * t)
                    if s == 0 and not last:
                        stats3(t + 1)
                    dve.wait_ge(u3_hi, n + 1)
                    dve.tensor_tensor(u3l[:], hh[:], u3h[:].bitcast(F32), ALU.subtract).then_inc(u3_lo, 1)
                    if s == 0 and not last:
                        norm3(t + 1)
                    if s == 0:
                        for piece in fresh[4 * SETS:]:
                            split_pieces(dve, piece, piece + 1, False)

            for step3 in SCHEDULE3:
                run3(dve, tile3, *step3)
            add_down(16 * HALVES * TILES, SETS * HALVES * TILES)

        @block.tensor
        def _(pe):
            def hT_turn(t):
                pe.wait_ge(h_ok, t + 1)
                for k in range(KC):
                    ins = pe.transpose(ps[:, 7, k * P:k * P + P], h[:, k * P:k * P + P], ident)
                ins.then_inc(hT_ps, 1)

            def project(bank, piece, wide, col, weights=False):
                for k in range(KC):
                    at = piece + (k // 2 if wide == 512 else k)
                    lo = (k % 2) * 512 if wide == 512 else col
                    if weights:
                        pe.wait_ge(w_lo, at + 1)
                    ins = mm3(pe, ps[:, bank], hTh[:, k], hTl[:, k], *place(1, at, lo, 512), k == 0, k == KC - 1)
                return ins

            def onT_turn():
                for j in range(H):
                    ins = pe.transpose(ps[:, 4 + j // 4, (j % 4) * P:(j % 4) * P + P], sc[:, j], ident)
                    if j % 4 == 3:
                        ins.then_inc(onT_ps, 1)

            def out_project():
                for j in range(H):
                    at, lo = O0 + j // 2, (j % 2) * 512
                    ins = mm3(pe, ps[:, 6], onTh[:, j], onTl[:, j], *place(1, at, lo, 512), j == 0, j == H - 1)
                ins.then_inc(attn_ps, 1)

            def step(t, first, last):
                pe.wait_ge(hT_lo, t + 1)
                project(0, Q0, 512, 0, first)
                project(1, K0, 512, 0, first).then_inc(qk_ps, 1)
                if not first:
                    pe.wait_ge(on_ok, t)
                    onT_turn()
                for j in range(2):
                    ins = project(2 + j, V0, 1024, 512 * j, first)
                ins.then_inc(v_ps, 1)
                if not first:
                    pe.wait_ge(onT_lo, 2 * t)
                    pe.wait_ge(state_sum, t)
                    out_project()
                pe.wait_ge(qk_ok, t + 1)
                qkv = qk[:].rearrange("p h d -> p (h d)")
                for j in range(2 * PAIRS):
                    ins = pe.transpose(ps[:, j // PAIRS, (j % PAIRS) * P:(j % PAIRS) * P + P],
                                       qkv[:, j * P:j * P + P], ident)
                    if j % PAIRS == PAIRS - 1:
                        ins.then_inc(qkT_ps, 1)
                project(4, G0, 1024, 0, first).then_inc(g_ps, 1)
                pe.wait_ge(kT_ok, t + 1)
                pe.wait_ge(qT_ok, 2 * t + 2)
                for r in range(PAIRS):
                    ins = pe.matmul(ps[:, r // 2, (r % 2) * 256:(r % 2) * 256 + 256], kT[:, r],
                                    qbd[:, r].rearrange("p a i -> p (a i)"), start=True, stop=True)
                ins.then_inc(s_ps, 1)
                project(5, G0, 1024, 512, first).then_inc(g_ps, 1)
                if not last:
                    hT_turn(t + 1)
                pe.wait_ge(s_ok, t + 1)
                pe.wait_ge(v_ok, t + 1)
                pe.wait_ge(state_ok, t + 1)
                b = t % B
                for j in range(H):
                    o = ps[:, 2 + j // 4, (j % 4) * DV:(j % 4) * DV + DV]
                    if isinstance(t, int):
                        s_in = state[:, b, (j // 2) * DV:(j // 2) * DV + DV]
                    else:
                        s_in = state[:, bass.ds(b, 1), (j // 2) * DV:(j // 2) * DV + DV].rearrange("p a n -> p (a n)")
                    pe.matmul(o, sc[:, j], v[:, j], start=True, stop=False)
                    ins = pe.matmul(o, qbd[:, j // 2, j % 2], s_in, start=False, stop=True)
                ins.then_inc(o_ps, 1)
                if last:
                    return
                if not first:
                    pe.wait_ge(x2_ok, t)
                for j in range(H):
                    ins = pe.matmul(ps[64 * (j % 2):64 * (j % 2) + 64, 6, (j // 2) * DV:(j // 2) * DV + DV],
                                    qk[:, H + j], v[:, j], start=True, stop=True)
                ins.then_inc(u_ps, 1)

            pe.wait_ge(consts_in, 80)
            hT_turn(0)
            step(0, True, False)
            pe.wait_ge(w_lo, NP1)
            with pe.Fori(1, STEPS - 1) as t:
                step(t, False, False)
            step(STEPS - 1, False, True)
            pe.wait_ge(on_ok, STEPS)
            onT_turn()
            pe.wait_ge(onT_lo, 2 * STEPS)
            pe.wait_ge(state_sum, STEPS - 1)
            out_project()

            def h2T_turn(k, bank):
                for s in range(SUB):
                    ins = pe.transpose(ps[:, bank, s * P:s * P + P], h2[:, s, k * P:k * P + P], ident)
                ins.then_inc(h2T_ps, 1)

            def up2(t, f, weights):
                if weights:
                    pe.wait_ge(w_lo, NP1 + f + f // 2 + 1)
                if f >= 2:
                    pe.wait_ge(u2_ok, FT * t + f - 1)
                for g in range(2):
                    for k in range(KC):
                        lo = 512 * g + P * k
                        ins = mm3(pe, ps[:, 4 + 2 * (f % 2) + g], *place(2, f, lo, P), h2Th[:, k], h2Tl[:, k],
                                  k == 0, k == KC - 1)
                ins.then_inc(up2_ps, 1)

            def down2_add(t, f, weights):
                if weights:
                    pe.wait_ge(w_lo, min(NP1 + 3 * (f // 2) + 3, ENDS[1]))
                pe.wait_ge(u2_lo, FT * t + f + 1)
                if f == 0 and (not isinstance(t, int) or t > 0):
                    pe.wait_ge(y_ok, SUB * t)
                for s in range(SUB):
                    ins = mm3(pe, ps[:, s], u2h[:, f % 2, s * P:s * P + P], u2l[:, f % 2, s * P:s * P + P],
                              *place(2, FT + f // 2, 512 * (f % 2), 512), f == 0, f == FT - 1)
                ins.then_inc(down2, 1)

            def tile2(t, first, last):
                pe.wait_ge(h2T_lo, KC * t + KC)
                for f in range(FT):
                    up2(t, f, first)
                    if f == FT - 1:
                        if last:
                            pe.wait_ge(xn_ok, SUB)
                        else:
                            pe.wait_ge(h2_ok, SUB * t + 2 * SUB)
                        pe.wait_ge(u2_ok, FT * t + FT - 1)
                        h2T_turn(0, 6)
                        h2T_turn(1, 7)
                    if f:
                        down2_add(t, f - 1, first)
                pe.wait_ge(u2_ok, FT * t + FT)
                h2T_turn(2, 4)
                h2T_turn(3, 5)
                down2_add(t, FT - 1, first)

            pe.wait_ge(h2_ok, SUB)
            for k, bank in enumerate(h2T_banks(0)):
                if bank == 6:
                    pe.wait_ge(x2_ok, STEPS)
                h2T_turn(k, bank)
            tile2(0, True, False)
            with pe.Fori(1, TILES - 1) as t:
                tile2(t, False, False)
            tile2(TILES - 1, False, True)

            def up3(t, s, m, weights):
                n = 4 * (SETS * t + s) + m
                if s or m >= 2:
                    pe.wait_ge(hh_ok, n - 1)
                for g in range(2):
                    for k in range(KC):
                        at, lo = 4 * s + 2 * g + k // 2, 512 * (k % 2) + P * m
                        if weights and m == 0:
                            pe.wait_ge(w_lo, weights + at + 1)
                        ins = mm3(pe, ps[:, 4 + 2 * (m % 2) + g], *place(3, at, lo, P), h2Th[:, k], h2Tl[:, k],
                                  k == 0, k == KC - 1)
                ins.then_inc(up3_ps, 1)

            def down3_add(s, members, done):
                for m in members:
                    for j in range(SUB):
                        ins = mm3(pe, ps[:, j], u3h[:, m, j * P:j * P + P], u3l[:, m, j * P:j * P + P],
                                  *place(3, 4 * SETS + 2 * s + m // 2, 512 * (m % 2), 512),
                                  s == 0 and m == 0, s == SETS - 1 and m == 3)
                if done:
                    ins.then_inc(down3, 1)

            def tile3(t, first=False, last=False, fresh=()):
                weights = ENDS[1] if first else ENDS[2] if isinstance(t, int) and t == TILES else 0
                pe.wait_ge(h2T_lo, KC * (t + TILES) + KC)
                for m in range(4):
                    up3(t, 0, m, weights)
                if not first:
                    pe.wait_ge(u3_lo, SETS * t)
                    down3_add(1, range(4), True)
                for m in range(4):
                    up3(t, 1, m, weights)
                if weights:
                    pe.wait_ge(w_lo, weights + NP3)
                if not last:
                    pe.wait_ge(xn_ok, SUB * t + 2 * SUB)
                    pe.wait_ge(hh_ok, 4 * SETS * t + 4 * SETS - 1)
                    h2T_turn(0, 4)
                    h2T_turn(1, 5)
                pe.wait_ge(u3_lo, SETS * t + 1)
                if first:
                    pe.wait_ge(y_ok, SUB * TILES)
                else:
                    pe.wait_ge(acc_ok, SUB * t)
                down3_add(0, range(0, 2), False)
                if not last:
                    pe.wait_ge(hh_ok, 4 * SETS * t + 4 * SETS)
                    h2T_turn(2, 6)
                    h2T_turn(3, 7)
                down3_add(0, range(2, 4), True)

            for step3 in SCHEDULE3:
                run3(pe, tile3, *step3)
            pe.wait_ge(u3_lo, SETS * HALVES * TILES)
            down3_add(1, range(4), True)


_INS = ["hidden_states", "attn_norm_w", "q_w", "k_w", "v_w", "g_w", "o_w", "gnorm_w", "mlp_norm_w",
        "gate_w", "down_w"]
_FFN = ["w_gate", "w_up", "w_down"]


def _constants():
    import numpy as np

    f = np.float32
    inv = (f(1.0) / np.power(f(10000.0), np.arange(0, DK, 2, dtype=f) / f(DK))).astype(f)
    ang = (np.arange(L, dtype=f)[:, None] * inv).astype(f).astype(np.float64)
    cos, sin = np.cos(ang), np.sin(ang)
    by_chunk = lambda a: a.reshape(CH, P, DK).transpose(1, 0, 2).reshape(P, CH * DK)
    gamma = 1.0 - 2.0 ** (-5.0 - np.arange(H))
    i = np.arange(P)
    t = np.zeros((P, NCONST), np.float32)
    t[:, COS:COS + CH * DK] = by_chunk(np.concatenate([cos, cos], 1))
    t[:, SIN:SIN + CH * DK] = by_chunk(np.concatenate([-sin, sin], 1))
    t[:, DEC:DEC + H] = gamma[None] ** (i[:, None] + 1.0) * DK ** -0.5
    t[:, DEC + H:DEC + 2 * H] = gamma[None] ** -(i[:, None] + 1.0)
    for r in range(PAIRS):
        for a in range(2):
            t[64 * a:64 * a + 64, GAM + r * DV:GAM + (r + 1) * DV] = gamma[2 * r + a] ** P
    t[:, MASK:MASK + P] = i[:, None] <= i[None, :]
    t[:, IDN:IDN + P] = np.eye(P)
    return t


def kernel(**inputs):
    import numpy as _np
    import concourse.bacc as _bacc
    from concourse import mybir as _mybir
    from concourse.bass_utils import run_bass_kernel_spmd as _run

    nc = _bacc.Bacc("TRN2", target_bir_lowering=False, num_devices=1)
    arrays, args = {}, []
    named = [("L0_attn_" + n) for n in _INS] + [("L0_ffn_" + n) for n in _FFN]
    for name in named:
        arrays[name] = _np.ascontiguousarray(inputs[name])
    arrays["constants"] = _constants()
    for name, a in arrays.items():
        args.append(nc.dram_tensor(name, a.shape, _mybir.dt.from_np(a.dtype), kind="ExternalInput").ap())
    out = nc.dram_tensor("out_0", (B, L, D), _mybir.dt.float32, kind="ExternalOutput").ap()
    build_program(nc, *args, out)
    r = _run(nc, [arrays], core_ids=[0])
    return r.results[0]["out_0"]
```

```python
from contextlib import ExitStack

import concourse.bass as bass
from concourse import mybir

F32 = mybir.dt.float32
F32R = mybir.dt.float32r
BF16 = mybir.dt.bfloat16
ALU = mybir.AluOpType
ACT = mybir.ActivationFunctionType
AX_X = mybir.AxisListType.X

P = 128
B, L, D = 4, 1024, 512
H, DK, DV = 8, 64, 128
KC = D // P
CH = L // P
STEPS = B * CH
PAIRS = H // 2
INTER = 1408
FT = INTER // P
TOK = 512
SUB = TOK // P
TILES = B * L // TOK
HID = 2048
HALVES = 2
SETS = HID // HALVES // (4 * P)
LN_EPS, RMS_EPS = 1e-5, 1e-6

PIECE = 1024
NP1 = 16
NP2 = FT + (FT + 1) // 2
NP3 = 6 * SETS
KEPT = NP3
Q0, K0, V0, G0, O0 = 0, 2, 4, 8, 12
SLOTS = 4

COS, SIN, DEC, GAM, MASK, IDN, NCONST = 0, 512, 1024, 1040, 1552, 1680, 1808


def build_program(nc, x, attn_norm_w, q_w, k_w, v_w, g_w, o_w, gnorm_w, mlp_norm_w, gate_w, down_w,
                  f_gate_w, f_up_w, f_down_w, consts, out):
    x_rows = x.rearrange("b (c p) d -> (b c) p d", p=P)
    x_tiles = x.rearrange("b (t s p) d -> (b t) p s d", s=SUB, p=P)
    out_tiles = out.rearrange("b (t s p) d -> (b t) p s d", s=SUB, p=P)
    x2_dram = nc.dram_tensor("x2_dram", (B * L, D), F32, kind="Internal").ap()
    y_dram = nc.dram_tensor("y_dram", (B * L, D), F32, kind="Internal").ap()
    z_dram = nc.dram_tensor("z_dram", (B * L, D), F32, kind="Internal").ap()
    xTh_dram, xTl_dram = (nc.dram_tensor(n, (TILES, P, KC * TOK), F32, kind="Internal").ap()
                          for n in ("xTh_dram", "xTl_dram"))
    x2_rows = x2_dram.rearrange("(n p) d -> n p d", p=P)
    tiles_of = lambda a: a.rearrange("(t s p) d -> t p s d", s=SUB, p=P)
    x2_tiles, y_tiles, z_tiles = tiles_of(x2_dram), tiles_of(y_dram), tiles_of(z_dram)

    with ExitStack() as ctx:
        def sem(name):
            return ctx.enter_context(nc.semaphore(name))

        def sb(stack, name, shape, dt=F32):
            return stack.enter_context(nc.sbuf_tensor(name, shape, dt))

        ps = ctx.enter_context(nc.psum_tensor("ps", [P, 8, 512], F32))

        stage = sb(ctx, "stage", [P, SLOTS, PIECE])
        idn = sb(ctx, "idn", [P, P])
        norms = sb(ctx, "norms", [P, 2 * KC + 1])
        ssq = sb(ctx, "ssq", [P, SUB])
        sme = sb(ctx, "sme", [P, SUB])
        srs = sb(ctx, "srs", [P, SUB])
        st3 = sb(ctx, "st3", [P, SUB, 6])
        mv3 = sb(ctx, "mv3", [P, SUB, 2])
        ve3 = sb(ctx, "ve3", [P, SUB])
        rs3 = sb(ctx, "rs3", [P, SUB])
        pool_c = sb(ctx, "pool_c", [P, 3, 8])
        warm = sb(ctx, "warm", [P, 1])
        ident = idn[:]

        Wh = sb(ctx, "Wh", [P, KEPT, PIECE], F32R)
        Wl = sb(ctx, "Wl", [P, KEPT, PIECE], F32R)

        with ExitStack() as c1:
            tab = sb(c1, "tab", [P, IDN])
            hTh = sb(c1, "hTh", [P, KC, P], F32R)
            hTl = sb(c1, "hTl", [P, KC, P], F32R)
            xt = sb(c1, "xt", [P, D])
            qk = sb(c1, "qk", [P, 2 * H, DK])
            state = sb(c1, "state", [P, B, PAIRS * DV])
            qbd = sb(c1, "qbd", [P, PAIRS, 2, P])
            v = sb(c1, "v", [P, H, DV])
            sg = sb(c1, "sg", [P, H, DV])
            sc = sb(c1, "sc", [P, H, P])
            rs = sb(c1, "rs", [P, 2 * H, DK])
            rc = sb(c1, "rc", [P, 2 * H, DK])
            x1 = sb(c1, "x1", [P, 2, D])
            onTh = sb(c1, "onTh", [P, H, P], F32R)
            onTl = sb(c1, "onTl", [P, H, P], F32R)
            W1h = sb(c1, "W1h", [P, NP1 - KEPT, PIECE], F32R)
            W1l = sb(c1, "W1l", [P, NP1 - KEPT, PIECE], F32R)
            st = sb(c1, "st", [P, 6])
            mv = sb(c1, "mv", [P, 2])
            nrm = sb(c1, "nrm", [P, 6])
            oss = sb(c1, "oss", [P, H])
            ome = sb(c1, "ome", [P, H])
            ors = sb(c1, "ors", [P, H])
            rc_flat, rs_flat = (a[:].rearrange("p h d -> p (h d)") for a in (rc, rs))
            kT = rc_flat[:, 0:PAIRS * P].rearrange("p (r j) -> p r j", r=PAIRS)
            x2 = rc_flat[:, PAIRS * P:PAIRS * P + D]
            h = rs_flat[:, 0:D]

        x2t = sb(ctx, "x2t", [P, SUB, D])
        h2 = sb(ctx, "h2", [P, SUB, D])
        res = sb(ctx, "res", [P, SUB, D])
        h2Th = sb(ctx, "h2Th", [P, KC, TOK], F32R)
        h2Tl = sb(ctx, "h2Tl", [P, KC, TOK], F32R)
        sg2 = sb(ctx, "sg2", [P, 2, TOK])
        with ExitStack() as c2:
            W2h = sb(c2, "W2h", [P, 2 * (NP2 - KEPT) - FT % 2, PIECE // 2], F32R)
            W2l = sb(c2, "W2l", [P, 2 * (NP2 - KEPT) - FT % 2, PIECE // 2], F32R)
            u2 = sb(c2, "u2", [P, 2, TOK])
            u2h = sb(c2, "u2h", [P, 2, TOK], F32R)
            u2l = sb(c2, "u2l", [P, 2, TOK], F32R)
        with ExitStack() as c3:
            hh = sb(c3, "hh", [P, 4, TOK])
            ab = sb(c3, "ab", [P, 4, TOK])
            cmp = sb(c3, "cmp", [P, 6, TOK], BF16)
            win = sb(c3, "win", [P, 4, TOK], BF16)
            u3h = sb(c3, "u3h", [P, 4, TOK], F32R)
            u3l = sb(c3, "u3l", [P, 4, TOK], F32R)

        consts_in = sem("consts_in")
        tab_in = sem("tab_in")
        pool_c_set = sem("pool_c_set")
        staged = [sem(f"staged{i}") for i in range(SLOTS)]
        w_hi = sem("w_hi")
        w_lo = sem("w_lo")
        x_in = sem("x_in")
        stat = sem("stat")
        mean_var = sem("mean_var")
        nrm_chain = sem("nrm_chain")
        rstd_ok = sem("rstd_ok")
        x1_ok = sem("x1_ok")
        h_ok = sem("h_ok")
        hT_ps = sem("hT_ps")
        hT_hi = sem("hT_hi")
        hT_lo = sem("hT_lo")
        qk_ps = sem("qk_ps")
        rope_prod = sem("rope_prod")
        rope_sum = sem("rope_sum")
        qk_ok = sem("qk_ok")
        qkT_ps = sem("qkT_ps")
        kT_ok = sem("kT_ok")
        qT_ok = sem("qT_ok")
        qbd_zero = sem("qbd_zero")
        v_ps = sem("v_ps")
        v_ok = sem("v_ok")
        g_ps = sem("g_ps")
        sg_ok = sem("sg_ok")
        s_ps = sem("s_ps")
        s_ok = sem("s_ok")
        o_ps = sem("o_ps")
        osq_ok = sem("osq_ok")
        oss_ok = sem("oss_ok")
        ome_ok = sem("ome_ok")
        ors_ok = sem("ors_ok")
        og_ok = sem("og_ok")
        on_ok = sem("on_ok")
        onT_ps = sem("onT_ps")
        onT_hi = sem("onT_hi")
        onT_lo = sem("onT_lo")
        attn_ps = sem("attn_ps")
        x2_ok = sem("x2_ok")
        x2_out = sem("x2_out")
        u_ps = sem("u_ps")
        state_sum = sem("state_sum")
        state_ok = sem("state_ok")
        x2t_in = sem("x2t_in")
        xres_in = sem("xres_in")
        res_ok = sem("res_ok")
        ssq_ok = sem("ssq_ok")
        sme_ok = sem("sme_ok")
        srs_ok = sem("srs_ok")
        h2_ok = sem("h2_ok")
        h2T_ps = sem("h2T_ps")
        h2T_hi = sem("h2T_hi")
        h2T_lo = sem("h2T_lo")
        up2_ps = sem("up2_ps")
        sg2_ok = sem("sg2_ok")
        u2_ok = sem("u2_ok")
        u2_hi = sem("u2_hi")
        u2_lo = sem("u2_lo")
        down2 = sem("down2")
        y_ok = sem("y_ok")
        y_out = sem("y_out")
        yt_in = sem("yt_in")
        st3_ok = sem("st3_ok")
        mv3_ok = sem("mv3_ok")
        ve3_ok = sem("ve3_ok")
        rs3_ok = sem("rs3_ok")
        xn_ok = sem("xn_ok")
        up3_ps = sem("up3_ps")
        sg3_ok = sem("sg3_ok")
        hh_ok = sem("hh_ok")
        ab_ok = sem("ab_ok")
        cmp_ok = sem("cmp_ok")
        win_ok = sem("win_ok")
        win2_ok = sem("win2_ok")
        kept = sem("kept")
        u3_hi = sem("u3_hi")
        u3_lo = sem("u3_lo")
        down3 = sem("down3")
        xT_out = sem("xT_out")
        xT_in = sem("xT_in")
        acc_in = sem("acc_in")
        acc_ok = sem("acc_ok")
        acc_out = sem("acc_out")

        def place(phase, at, lo, width):
            if at < KEPT:
                return Wh[:, at, lo:lo + width], Wl[:, at, lo:lo + width]
            two = (W1h, W1l) if phase == 1 else (W2h, W2l)
            if phase == 1:
                return tuple(w[:, at - KEPT, lo:lo + width] for w in two)
            half, lo = 2 * (at - KEPT) + lo // 512, lo % 512
            if width <= 512:
                return tuple(w[:, half, lo:lo + width] for w in two)
            return tuple(w[:, half:half + 2].rearrange("p a n -> p (a n)") for w in two)

        def rows2(w, j, cols=slice(None)):
            return w.rearrange("(a p) n -> p a n", p=P)[:, 2 * j:2 * j + 2, cols]

        def pieces():
            for w, first in ((q_w, Q0), (k_w, K0)):
                for j in range(2):
                    yield [(0, rows2(w, j))], [(512 * a, 512, 2 * j + a) for a in range(2)], 1, first + j
            for w, first in ((v_w, V0), (g_w, G0)):
                for kc in range(KC):
                    yield ([(0, w.rearrange("(a p) n -> p a n", p=P)[:, kc:kc + 1, :])],
                           [(0, 1024, kc)], 1, first + kc)
            for j in range(4):
                yield [(0, rows2(o_w, j))], [(0, 1024, 2 * KC)], 1, O0 + j
            gate = gate_w.rearrange("(a p) n -> p a n", p=P)
            down = down_w.rearrange("(f p) n -> p f n", p=P)
            for f in range(FT):
                yield ([(512 * g, gate[:, :, g * INTER + f * P:g * INTER + f * P + P]) for g in range(2)],
                       [(P * kc, P, KC + kc) for kc in range(KC)], 2, f)
                if f % 2 or f == FT - 1:
                    n = f % 2 + 1
                    yield [(0, down[:, f + 1 - n:f + 1, :])], [(0, 512 * n, None)], 2, FT + f // 2
            fdown = f_down_w.rearrange("(g p r) n -> g p r n", p=P, r=4)
            for half in range(HALVES):
                for s in range(SETS):
                    c0 = (half * SETS + s) * 512
                    for w, k in ((f_gate_w, 0), (f_up_w, 2)):
                        for j in range(2):
                            yield [(0, rows2(w, j, slice(c0, c0 + 512)))], "group", 3, 4 * s + k + j
                for s in range(SETS):
                    for j in range(2):
                        yield ([(0, fdown[half * SETS + s][:, 2 * j:2 * j + 2, :])],
                               [(0, 1024, None)], 3, 4 * SETS + 2 * s + j)

        PIECES = list(pieces())
        ENDS = [NP1, NP1 + NP2, NP1 + NP2 + NP3, NP1 + NP2 + 2 * NP3]
        assert len(PIECES) == ENDS[-1]
        loads_before = [sum(len(PIECES[m][0]) for m in range(n + 1) if m % SLOTS == n % SLOTS)
                        for n in range(len(PIECES))]

        def need(eng, s, n):
            if not isinstance(n, int) or n > 0:
                eng.wait_ge(s, n)

        def load_pieces(eng, first, end):
            for n in range(first, end):
                need(eng, w_lo, n - SLOTS + 1)
                for col, src in PIECES[n][0]:
                    width = src.shape[1] * src.shape[2]
                    dst = stage[:, n % SLOTS, col:col + width].rearrange("p (a n) -> p a n", a=src.shape[1])
                    eng.dma_start(dst, src).then_inc(staged[n % SLOTS], 16)

        def split_pieces(eng, first, end, hi):
            for n in range(first, end):
                loads, parts, phase, at = PIECES[n]
                raw = stage[:, n % SLOTS]
                eng.wait_ge(staged[n % SLOTS], 16 * loads_before[n])
                if not hi:
                    eng.wait_ge(w_hi, n + 1)
                if parts == "group":
                    for a in range(2):
                        src = raw[:, 512 * a:512 * a + 512].rearrange("p (g r) -> p r g", r=4)
                        dh, dl = (w.rearrange("p (r g) -> p r g", r=4) for w in place(phase, at, 512 * a, 512))
                        if hi:
                            ins = eng.copy(dh, src)
                        else:
                            ins = eng.tensor_tensor(dl, src, dh.bitcast(F32), ALU.subtract)
                else:
                    for col, width, norm in parts:
                        scale = norms[:, norm:norm + 1] if norm is not None else 1.0
                        src = raw[:, col:col + width]
                        dh, dl = place(phase, at, col, width)
                        if phase == 2 and at < FT:
                            src = raw.rearrange("p (g n) -> p g n", g=2)[:, :, col:col + width]
                            dh, dl = (w.rearrange("p (g n) -> p g n", g=2)[:, :, col:col + width]
                                      for w in place(phase, at, 0, PIECE))
                        if hi:
                            ins = eng.activation(dh, src, ACT.Copy, scale=scale)
                        else:
                            ins = eng.scalar_tensor_tensor(out=dl, in0=src, scalar=scale, in1=dh.bitcast(F32),
                                                           op0=ALU.mult, op1=ALU.subtract)
                ins.then_inc(w_hi if hi else w_lo, 1)

        def mm3(pe, dst, lh, ll, rh, rl, start, stop):
            pe.matmul(dst, lh, rh, start=start, stop=False)
            pe.matmul(dst, lh, rl, start=False, stop=False)
            return pe.matmul(dst, ll, rh, start=False, stop=stop)

        def row_tile(t):
            return (t % B) * CH + t // B

        def due2(f):
            upto = lambda f: min(NP2, 3 * (f + 2) // 2 + 3)
            return NP1 + (upto(f - 1) if f else 4), NP1 + max(upto(f), 4)

        def h2T_banks(t):
            return (7, 4, 5, 3) if isinstance(t, int) and t == 0 else (6, 7, 4, 5)

        t1 = TILES
        NEW = range(ENDS[2], ENDS[3])
        SCHEDULE3 = [((0,), dict(first=True, norm=True)), ((1, t1 - 1), dict(norm=True)),
                     ((t1 - 1,), dict(fetch=True, fresh=[None] * 4 + list(NEW[0:4]))),
                     ((t1,), dict(fetch=True, fresh=NEW[4:12])),
                     ((t1 + 1, 2 * t1 - 1), dict(fetch=True)), ((2 * t1 - 1,), dict(last=True))]
        MEMBERS = (0, 1, 3, 2)

        def run3(eng, tile, turns, how):
            if len(turns) == 1:
                tile(turns[0], **how)
            else:
                with eng.Fori(*turns) as t:
                    tile(t, **how)

        def tile_at(a, i):
            return a[bass.ds(i, 1)].rearrange("a p s d -> p (a s) d")

        block = ctx.enter_context(nc.Block())

        @block.sync
        def _(sp):
            sp.dma_start(xt[:], x_rows[row_tile(0)]).then_inc(x_in, 16)
            sp.dma_start(norms[:, 0:KC], attn_norm_w.rearrange("(k p) -> p k", p=P), allow_slow_non_contiguous=True).then_inc(consts_in, 16)
            sp.dma_start(idn[:], consts[:, IDN:IDN + P]).then_inc(consts_in, 16)
            load_pieces(sp, 0, 4)
            sp.dma_start(tab[:], consts[:, 0:IDN]).then_inc(tab_in, 16)
            sp.dma_start(norms[:, KC:2 * KC], mlp_norm_w.rearrange("(k p) -> p k", p=P), allow_slow_non_contiguous=True).then_inc(tab_in, 16)
            sp.dma_start(norms[:, 2 * KC:2 * KC + 1], gnorm_w.rearrange("(p k) -> p k", k=1), allow_slow_non_contiguous=True).then_inc(tab_in, 16)
            sp.wait_ge(x1_ok, 1)
            sp.dma_start(xt[:], x_rows[row_tile(1)]).then_inc(x_in, 16)
            load_pieces(sp, 4, NP1)
            sp.wait_ge(x1_ok, 2)
            sp.dma_start(xt[:], x_rows[row_tile(2)]).then_inc(x_in, 16)

            def row_at(a, t):
                return a[bass.ds(row_tile(t), 1)].rearrange("a p d -> p (a d)")

            def load_x(t):
                sp.wait_ge(x1_ok, t)
                sp.dma_start(xt[:], row_at(x_rows, t)).then_inc(x_in, 16)

            def store_x2(t):
                sp.wait_ge(x2_ok, t + 1)
                sp.dma_start(row_at(x2_rows, t), x2).then_inc(x2_out, 16)

            with sp.Fori(0, STEPS - 3) as t:
                store_x2(t)
                load_x(t + 3)
            load_pieces(sp, NP1, NP1 + SLOTS)
            for t in range(STEPS - 3, STEPS - 1):
                sp.wait_ge(x2_ok, t + 1)
                sp.dma_start(x2_rows[row_tile(t)], x2).then_inc(x2_out, 16)

            sp.wait_ge(o_ps, STEPS)
            sp.dma_start(x2t[:], x2_tiles[0]).then_inc(x2t_in, 16)
            sp.dma_start(res[:], x_tiles[0]).then_inc(xres_in, 16)
            sp.wait_ge(x2_ok, STEPS)
            sp.dma_start(x2_rows[row_tile(STEPS - 1)], x2).then_inc(x2_out, 16)
            load_pieces(sp, NP1 + SLOTS, NP1 + 9)
            sp.wait_ge(res_ok, 1)
            sp.wait_ge(x2_out, 16 * STEPS)
            sp.dma_start(x2t[:], x2_tiles[1]).then_inc(x2t_in, 16)
            load_pieces(sp, NP1 + 9, ENDS[1])
            with sp.Fori(3, TILES + 1) as i:
                sp.wait_ge(y_ok, SUB * (i - 2))
                sp.dma_start(tile_at(y_tiles, i - 3), res[:]).then_inc(y_out, 16)
                sp.wait_ge(y_out, 16 * (i - 2))
                sp.dma_start(res[:], tile_at(x_tiles, i - 2)).then_inc(xres_in, 16)
                sp.wait_ge(res_ok, i - 1)
                sp.dma_start(x2t[:], tile_at(x2_tiles, i - 1)).then_inc(x2t_in, 16)
            t = TILES - 2
            sp.wait_ge(y_ok, SUB * (t + 1))
            sp.dma_start(y_tiles[t], res[:]).then_inc(y_out, 16)
            sp.wait_ge(y_out, 16 * (t + 1))
            sp.dma_start(res[:], x_tiles[t + 1]).then_inc(xres_in, 16)

            load_pieces(sp, ENDS[1], ENDS[1] + SLOTS)
            sp.wait_ge(res_ok, TILES)
            sp.dma_start(x2t[:], y_tiles[0]).then_inc(yt_in, 16)
            load_pieces(sp, ENDS[1] + SLOTS, ENDS[2])
            sp.wait_ge(xn_ok, SUB)
            sp.dma_start(x2t[:], y_tiles[1]).then_inc(yt_in, 16)
            sp.wait_ge(y_ok, SUB * TILES)
            sp.dma_start(y_tiles[TILES - 1], res[:]).then_inc(y_out, 16)
            sp.wait_ge(y_out, 16 * TILES)
            sp.dma_start(res[:], y_tiles[0]).then_inc(acc_in, 16)

            def flat_tile(a, tile):
                return a[tile] if isinstance(tile, int) else a[bass.ds(tile, 1)].rearrange("a p n -> p (a n)")

            def store_xT(t):
                sp.wait_ge(h2T_lo, KC * (t + TILES + 1))
                for dram, part in ((xTh_dram, h2Th), (xTl_dram, h2Tl)):
                    src = part[:].rearrange("p k t -> p (k t)").bitcast(F32)
                    sp.dma_start(flat_tile(dram, t), src).then_inc(xT_out, 16)

            def fetch_xT(t, tile):
                sp.wait_ge(h2T_lo, KC * (t + TILES))
                for dram, dst in ((xTh_dram, x2t), (xTl_dram, h2)):
                    sp.dma_start(dst[:].rearrange("p s d -> p (s d)"), flat_tile(dram, tile)).then_inc(xT_in, 16)

            def store_sum(t):
                src, dst = (y_tiles, z_tiles) if t < TILES else (z_tiles, out_tiles)
                sp.wait_ge(acc_ok, SUB * (t + 1))
                sp.dma_start(dst[t % TILES], res[:]).then_inc(acc_out, 16)
                sp.wait_ge(acc_out, 16 * (t + 1))
                if t < HALVES * TILES - 1:
                    src = y_tiles if t + 1 < TILES else z_tiles
                    sp.dma_start(res[:], src[(t + 1) % TILES]).then_inc(acc_in, 16)

            store_xT(0)
            with sp.Fori(3, TILES + 1) as i:
                sp.wait_ge(xn_ok, SUB * (i - 1))
                sp.dma_start(x2t[:], tile_at(y_tiles, i - 1)).then_inc(yt_in, 16)
                store_xT(i - 2)
                sp.wait_ge(acc_ok, SUB * (i - 2))
                sp.dma_start(tile_at(z_tiles, i - 3), res[:]).then_inc(acc_out, 16)
                sp.wait_ge(acc_out, 16 * (i - 2))
                sp.dma_start(res[:], tile_at(y_tiles, i - 2)).then_inc(acc_in, 16)
            t = TILES - 1
            store_xT(t)
            sp.wait_ge(xT_out, 32 * TILES)
            fetch_xT(t + 1, 0)
            load_pieces(sp, ENDS[2], ENDS[2] + SLOTS)
            store_sum(t - 1)
            load_pieces(sp, ENDS[2] + SLOTS, ENDS[2] + 2 * SLOTS)
            fetch_xT(t + 2, 1)
            load_pieces(sp, ENDS[2] + 2 * SLOTS, ENDS[3])
            store_sum(t)
            with sp.Fori(3, TILES + 1) as i:
                fetch_xT(i + (TILES - 1), i - 1)
                sp.wait_ge(acc_ok, SUB * (i + (TILES - 2)))
                sp.dma_start(tile_at(out_tiles, i - 3), res[:]).then_inc(acc_out, 16)
                sp.wait_ge(acc_out, 16 * (i + (TILES - 2)))
                sp.dma_start(res[:], tile_at(z_tiles, i - 2)).then_inc(acc_in, 16)
            store_sum(2 * TILES - 2)
            done = 2 * TILES - 1
            for s in range(SUB):
                sp.wait_ge(acc_ok, SUB * done + s + 1)
                sp.dma_start(out_tiles[TILES - 1][:, s], res[:, s]).then_inc(acc_out, 16)
            sp.wait_ge(acc_out, 16 * (done + SUB))

        @block.gpsimd
        def _(pool):
            for at, value in enumerate((-0.5, LN_EPS, RMS_EPS)):
                pool.memset(pool_c[:, at], value).then_inc(pool_c_set, 1)
            pool.memset(qbd[:], 0.0).then_inc(qbd_zero, 1)
            pool.wait_ge(pool_c_set, 3)
            minus_half, ln_eps, rms_eps = (pool_c[:, at] for at in range(3))

            def norm_scalars(t):
                var, ve, rstd, vr, vrr, vrre, r2 = mv[:, 1:2], *(nrm[:, i:i + 1] for i in range(6))
                pool.wait_ge(mean_var, t + 1)
                need(pool, h_ok, t)
                pool.tensor_tensor(ve, var, ln_eps[:, 0:1], ALU.add).then_inc(nrm_chain, 1)
                pool.wait_ge(nrm_chain, 4 * t + 1)
                pool.tensor_tensor(rstd, ve, minus_half[:, 0:1], ALU.pow).then_inc(rstd_ok, 1)
                pool.wait_ge(rstd_ok, 2 * t + 1)
                pool.tensor_tensor(vr, var, rstd, ALU.mult).then_inc(nrm_chain, 1)
                pool.wait_ge(nrm_chain, 4 * t + 2)
                pool.tensor_tensor(vrr, vr, rstd, ALU.mult).then_inc(nrm_chain, 1)
                pool.wait_ge(nrm_chain, 4 * t + 3)
                pool.tensor_tensor(vrre, vrr, rms_eps[:, 0:1], ALU.add).then_inc(nrm_chain, 1)
                pool.wait_ge(nrm_chain, 4 * t + 4)
                pool.tensor_tensor(r2, vrre, minus_half[:, 0:1], ALU.pow).then_inc(rstd_ok, 1)

            def head_scalars(t):
                pool.wait_ge(oss_ok, t + 1)
                pool.tensor_tensor(ome[:], oss[:], rms_eps, ALU.add).then_inc(ome_ok, 1)
                pool.wait_ge(ome_ok, t + 1)
                pool.tensor_tensor(ors[:], ome[:], minus_half, ALU.pow).then_inc(ors_ok, 1)

            norm_scalars(0)
            norm_scalars(1)
            head_scalars(0)
            with pool.Fori(1, STEPS - 1) as t:
                norm_scalars(t + 1)
                head_scalars(t)
            head_scalars(STEPS - 1)

            def rms_scalars(t):
                pool.wait_ge(ssq_ok, SUB * t + SUB)
                pool.tensor_tensor(sme[:], ssq[:], rms_eps[:, 0:SUB], ALU.add).then_inc(sme_ok, 1)
                pool.wait_ge(sme_ok, t + 1)
                pool.tensor_tensor(srs[:], sme[:], minus_half[:, 0:SUB], ALU.pow).then_inc(srs_ok, 1)

            def residual(t):
                pool.wait_ge(xres_in, 16 * t + 16)
                pool.wait_ge(x2t_in, 16 * t + 16)
                pool.wait_ge(h2_ok, SUB * t + SUB)
                pool.tensor_tensor(res[:], res[:], x2t[:], ALU.add).then_inc(res_ok, 1)

            rms_scalars(0)
            residual(0)
            with pool.Fori(1, TILES) as t:
                rms_scalars(t)
                residual(t)

            with pool.Fori(0, TILES) as t:
                pool.wait_ge(mv3_ok, SUB * t + SUB)
                pool.tensor_tensor(ve3[:], mv3[:, :, 1], ln_eps[:, 0:SUB], ALU.add).then_inc(ve3_ok, 1)
                pool.wait_ge(ve3_ok, t + 1)
                pool.tensor_tensor(rs3[:], ve3[:], minus_half[:, 0:SUB], ALU.pow).then_inc(rs3_ok, 1)

        @block.scalar
        def _(act):
            def make_h(t):
                act.wait_ge(x1_ok, t + 1)
                act.wait_ge(rstd_ok, 2 * t + 2)
                slot = x1[:, t % 2] if isinstance(t, int) else x1[:, bass.ds(t % 2, 1)].rearrange("p a d -> p (a d)")
                act.activation(h, slot, ACT.Copy, scale=nrm[:, 5:6]).then_inc(h_ok, 1)

            def hT_round(t):
                act.wait_ge(hT_ps, t + 1)
                act.copy(hTh[:].rearrange("p k t -> p (k t)"), ps[:, 7]).then_inc(hT_hi, 1)

            def onT_round(t):
                for j in range(2):
                    act.wait_ge(onT_ps, 2 * t + j + 1)
                    act.copy(onTh[:, 4 * j:4 * j + 4].rearrange("p h t -> p (h t)"), ps[:, 4 + j]).then_inc(onT_hi, 1)

            def step(t, first, last):
                if not first:
                    for j in range(2):
                        act.wait_ge(onT_ps, 2 * t + j - 1)
                        act.copy(onTh[:, 4 * j:4 * j + 4].rearrange("p h t -> p (h t)"), ps[:, 4 + j]).then_inc(onT_hi, 1)
                if first:
                    split_pieces(act, 8, 11, True)
                act.wait_ge(v_ps, t + 1)
                act.copy(v[:].rearrange("p h e -> p (h e)"), ps[:, 2:4].rearrange("p a n -> p (a n)")).then_inc(v_ok, 1)
                if first:
                    split_pieces(act, 11, 12, True)
                act.wait_ge(qkT_ps, 2 * t + 1)
                qT = ps[:, 0].rearrange("p (r i) -> p r i", r=PAIRS)
                if first:
                    act.wait_ge(qbd_zero, 1)
                act.copy(qbd[0:64, :, 0], qT[0:64]).then_inc(qT_ok, 1)
                act.copy(qbd[64:128, :, 1], qT[64:128]).then_inc(qT_ok, 1)
                act.wait_ge(qkT_ps, 2 * t + 2)
                act.copy(kT.rearrange("p r j -> p (r j)"), ps[:, 1]).then_inc(kT_ok, 1)
                act.wait_ge(g_ps, 2 * t + 1)
                act.activation(sg[:, 0:4].rearrange("p h e -> p (h e)"), ps[:, 4], ACT.Silu).then_inc(sg_ok, 1)
                if not last:
                    make_h(t + 1)
                if first:
                    act.wait_ge(tab_in, 48)
                    split_pieces(act, 12, 14, True)
                act.wait_ge(g_ps, 2 * t + 2)
                act.activation(sg[:, 4:8].rearrange("p h e -> p (h e)"), ps[:, 5], ACT.Silu).then_inc(sg_ok, 1)
                if not last:
                    hT_round(t + 1)
                if first:
                    split_pieces(act, 14, NP1, True)
                act.wait_ge(o_ps, t + 1)
                act.activation(rs[:].rearrange("p h e -> p (h e)"), ps[:, 2:4].rearrange("p a n -> p (a n)"),
                               ACT.Square, scale=DV ** -0.5).then_inc(osq_ok, 1)

            act.wait_ge(pool_c_set, 3)
            act.activation(warm[:], pool_c[:, 0, 0:1], ACT.Silu)
            make_h(0)
            act.wait_ge(consts_in, 32)
            split_pieces(act, 0, 1, True)
            hT_round(0)
            split_pieces(act, 1, 8, True)
            step(0, True, False)
            with act.Fori(1, STEPS - 1) as t:
                step(t, False, False)
            step(STEPS - 1, False, True)
            split_pieces(act, NP1, NP1 + 1, True)
            onT_round(STEPS - 1)

            def square_x2(t):
                act.wait_ge(x2t_in, 16 * t + 16)
                for s in range(SUB):
                    act.activation(h2[:, s], x2t[:, s], ACT.Square, scale=D ** -0.5,
                                   accum_out=ssq[:, s:s + 1]).then_inc(ssq_ok, 1)

            def make_h2(t):
                act.wait_ge(srs_ok, t + 1)
                for s in range(SUB):
                    act.activation(h2[:, s], x2t[:, s], ACT.Copy, scale=srs[:, s:s + 1]).then_inc(h2_ok, 1)

            def h2T_round(t):
                for k, bank in enumerate(h2T_banks(t)):
                    act.wait_ge(h2T_ps, KC * t + k + 1)
                    act.copy(h2Th[:, k], ps[:, bank]).then_inc(h2T_hi, 1)

            def tile2(t, first, last):
                for f in range(FT):
                    act.wait_ge(up2_ps, FT * t + f + 1)
                    act.activation(sg2[:, f % 2], ps[:, 4 + 2 * (f % 2)], ACT.Silu).then_inc(sg2_ok, 1)
                    act.wait_ge(u2_ok, FT * t + f + 1)
                    if f >= 2:
                        act.wait_ge(down2, FT * t + f - 1)
                    act.copy(u2h[:, f % 2], u2[:, f % 2]).then_inc(u2_hi, 1)
                    if first:
                        split_pieces(act, *due2(f), True)
                    if last and f:
                        split_pieces(act, ENDS[1] + f - 1, ENDS[1] + f, True)
                    if not last and f == 5:
                        square_x2(t + 1)
                    if not last and f == 6:
                        make_h2(t + 1)
                if not last:
                    h2T_round(t + 1)
                else:
                    split_pieces(act, ENDS[1] + FT - 1, ENDS[2] - 1, True)
                    h2T_round(TILES)
                    split_pieces(act, ENDS[2] - 1, ENDS[2], True)

            square_x2(0)
            split_pieces(act, NP1 + 1, NP1 + 2, True)
            make_h2(0)
            h2T_round(0)
            split_pieces(act, NP1 + 2, NP1 + 4, True)
            tile2(0, True, False)
            with act.Fori(1, TILES - 1) as t:
                tile2(t, False, False)
            tile2(TILES - 1, False, True)

            def xnT_round(t):
                for k in range(KC):
                    if k == 0:
                        act.wait_ge(xT_out, 32 * t)
                    act.wait_ge(h2T_ps, KC * (t + TILES) + k + 1)
                    act.copy(h2Th[:, k], ps[:, 4 + k]).then_inc(h2T_hi, 1)

            def xT_copy(t):
                act.wait_ge(xT_out, 32 * TILES)
                act.wait_ge(xT_in, 32 * (t - TILES + 1))
                for k in range(KC):
                    act.copy(h2Th[:, k], x2t[:, k]).then_inc(h2T_hi, 1)

            def tile3(t, first=False, norm=False, fetch=False, fresh=(), last=False):
                for s in range(SETS):
                    n = SETS * t + s
                    for m in range(4):
                        act.wait_ge(up3_ps, 4 * n + m + 1)
                        act.activation(sg2[:, m % 2], ps[:, 4 + 2 * (m % 2)], ACT.Silu).then_inc(sg3_ok, 1)
                        act.wait_ge(hh_ok, 4 * n + m + 1)
                        act.activation(ab[:, m], hh[:, m], ACT.Abs).then_inc(ab_ok, 1)
                        if fresh and fresh[4 * s + m] is not None:
                            split_pieces(act, fresh[4 * s + m], fresh[4 * s + m] + 1, True)
                    if s == 1 and norm:
                        xnT_round(t + 1)
                    if s == 1 and fetch:
                        xT_copy(t + 1)
                    if not (first and s == 0 or last and s == 1):
                        act.wait_ge(down3, n)
                    to = h2Th if last and s == 1 else u3h
                    for i, m in enumerate(MEMBERS):
                        act.wait_ge(kept, 4 * n + i + 1)
                        act.copy(to[:, m], hh[:, m]).then_inc(u3_hi, 1)

            for step3 in SCHEDULE3:
                run3(act, tile3, *step3)

        @block.vector
        def _(dve):
            def x1_slot(t):
                return x1[:, t % 2] if isinstance(t, int) else x1[:, bass.ds(t % 2, 1)].rearrange("p a d -> p (a d)")

            def stats(t):
                dve.wait_ge(x_in, 16 * t + 16)
                dve.bn_stats(st[:, 0:6], xt[:]).then_inc(stat, 1)

            def aggregate():
                dve.bn_aggr(mv[:], st[:, 0:6]).then_inc(mean_var, 1)

            def make_x1(t):
                dve.wait_ge(rstd_ok, 2 * t + 1)
                dve.tensor_scalar(x1_slot(t), xt[:], mv[:, 0:1], nrm[:, 1:2], ALU.subtract,
                                  ALU.mult).then_inc(x1_ok, 1)

            def hT_rest(t):
                dve.wait_ge(hT_hi, t + 1)
                dve.tensor_tensor(hTl[:].rearrange("p k t -> p (k t)"), ps[:, 7],
                                  hTh[:].rearrange("p k t -> p (k t)").bitcast(F32), ALU.subtract).then_inc(hT_lo, 1)

            def onT_rest(n):
                for j in range(2):
                    dve.wait_ge(onT_hi, n - 1 + j if isinstance(n, int) else n + (j - 1))
                    dve.tensor_tensor(onTl[:, 4 * j:4 * j + 4].rearrange("p h t -> p (h t)"), ps[:, 4 + j],
                                      onTh[:, 4 * j:4 * j + 4].rearrange("p h t -> p (h t)").bitcast(F32),
                                      ALU.subtract).then_inc(onT_lo, 1)

            def add_residual(t, made):
                dve.wait_ge(qk_ok, made + 1 if made < STEPS else made)
                dve.wait_ge(attn_ps, made)
                dve.tensor_tensor(x2, x1_slot(t), ps[:, 6], ALU.add).then_inc(x2_ok, 1)

            def step(t, first=False, last=False, update=True):
                c = t // B
                dve.wait_ge(qk_ps, t + 1)
                qkp = ps[:, 0:2].rearrange("p a (h d) -> p (a h) d", d=DK)
                cos = tab[:, COS:COS + CH * DK].rearrange("p (c d) -> p c d", d=DK)[:, bass.ds(c, 1), :]
                sin = tab[:, SIN:SIN + CH * DK].rearrange("p (c d) -> p c d", d=DK)[:, bass.ds(c, 1), :]
                hd = DK // 2
                if not isinstance(t, int) or t > 1:
                    dve.wait_ge(x2_out, 16 * (t - 1))
                dve.tensor_tensor(rc[:], qkp, cos.broadcast_to([P, 2 * H, DK]), ALU.mult).then_inc(rope_prod, 1)
                dve.tensor_tensor(rs[:, :, 0:hd], qkp[:, :, hd:DK],
                                  sin[:, :, 0:hd].broadcast_to([P, 2 * H, hd]), ALU.mult).then_inc(rope_prod, 1)
                dve.tensor_tensor(rs[:, :, hd:DK], qkp[:, :, 0:hd],
                                  sin[:, :, hd:DK].broadcast_to([P, 2 * H, hd]), ALU.mult).then_inc(rope_prod, 1)
                if not first:
                    onT_rest(2 * t)
                dve.wait_ge(rope_prod, 3 * t + 3)
                dve.tensor_tensor(rc[:], rc[:], rs[:], ALU.add).then_inc(rope_sum, 1)
                if not last:
                    stats(t + 1)
                    dve.wait_ge(stat, t + 2)
                dve.wait_ge(rope_sum, t + 1)
                dve.tensor_tensor(qk[:], rc[:], tab[:, DEC:DEC + 2 * H].rearrange("p (h a) -> p h a", a=1)
                                  .broadcast_to([P, 2 * H, DK]), ALU.mult).then_inc(qk_ok, 1)
                if first:
                    split_pieces(dve, 8, 12, False)
                if not last:
                    aggregate()
                if not first:
                    if isinstance(t, int):
                        add_residual(t - 1, t)
                    else:
                        add_residual_prev(t)
                if not last:
                    need(dve, x2_ok, t)
                    make_x1(t + 1)
                dve.wait_ge(s_ps, t + 1)
                dve.tensor_tensor(sc[:], ps[:, 0:2].rearrange("p a (h i) -> p (a h) i", i=P),
                                  tab[:, MASK:MASK + P].rearrange("p (a i) -> p a i", a=1).broadcast_to([P, H, P]),
                                  ALU.mult).then_inc(s_ok, 1)
                if not last:
                    hT_rest(t + 1)
                if first:
                    split_pieces(dve, 12, 14, False)
                dve.wait_ge(osq_ok, t + 1)
                dve.tensor_reduce(oss[:], rs[:].rearrange("p a d -> p (a d)").rearrange("p (h e) -> p h e", e=DV),
                                  AX_X, ALU.add).then_inc(oss_ok, 1)
                dve.wait_ge(sg_ok, 2 * t + 2)
                dve.tensor_tensor(sc[:], ps[:, 2:4].rearrange("p a (h e) -> p (a h) e", e=DV), sg[:],
                                  ALU.mult).then_inc(og_ok, 1)
                if update:
                    update_state(t)
                dve.wait_ge(ors_ok, t + 1)
                dve.wait_ge(og_ok, t + 1)
                dve.tensor_tensor(sc[:], sc[:], ors[:].rearrange("p (h a) -> p h a", a=1).broadcast_to([P, H, DV]),
                                  ALU.mult).then_inc(on_ok, 1)

            def update_state(t):
                b = t % B
                sb_ = state[:, b] if isinstance(t, int) else state[:, bass.ds(b, 1)].rearrange("p a n -> p (a n)")
                dve.wait_ge(u_ps, t + 1)
                dve.tensor_tensor(sb_, sb_, ps[:, 6], ALU.add).then_inc(state_sum, 1)
                dve.wait_ge(state_sum, t + 1)
                dve.tensor_tensor(sb_, sb_, tab[:, GAM:GAM + PAIRS * DV], ALU.mult).then_inc(state_ok, 1)

            def add_residual_prev(t):
                slot = x1[:, bass.ds((t + 1) % 2, 1)].rearrange("p a d -> p (a d)")
                dve.wait_ge(qk_ok, t + 1)
                dve.wait_ge(attn_ps, t)
                dve.tensor_tensor(x2, slot, ps[:, 6], ALU.add).then_inc(x2_ok, 1)

            dve.memset(state[:], 0.0).then_inc(state_ok, 1)
            stats(0)
            dve.wait_ge(stat, 1)
            aggregate()
            make_x1(0)
            dve.wait_ge(consts_in, 32)
            split_pieces(dve, 0, 1, False)
            hT_rest(0)
            split_pieces(dve, 1, 8, False)
            dve.wait_ge(state_ok, 1)
            dve.wait_ge(tab_in, 48)
            step(0, first=True)
            split_pieces(dve, 14, NP1, False)
            step(1)
            with dve.Fori(2, STEPS - B) as t:
                step(t)
            with dve.Fori(STEPS - B, STEPS - 1) as t:
                step(t, update=False)
            step(STEPS - 1, last=True, update=False)
            split_pieces(dve, NP1, NP1 + 1, False)
            onT_rest(2 * STEPS)
            split_pieces(dve, NP1 + 1, NP1 + 2, False)

            def stats3(t):
                dve.wait_ge(yt_in, 16 * t + 16)
                for s in range(SUB):
                    dve.bn_stats(st3[:, s], x2t[:, s]).then_inc(st3_ok, 1)
                dve.wait_ge(st3_ok, SUB * t + SUB)

            def aggregate3():
                for s in range(SUB):
                    dve.bn_aggr(mv3[:, s], st3[:, s]).then_inc(mv3_ok, 1)

            def norm3(t, parts):
                dve.wait_ge(rs3_ok, t + 1)
                for s in parts:
                    dve.tensor_scalar(h2[:, s], x2t[:, s], mv3[:, s, 0:1], rs3[:, s:s + 1], ALU.subtract,
                                      ALU.mult).then_inc(xn_ok, 1)

            def h2T_rest(t):
                for k, bank in enumerate(h2T_banks(t)):
                    dve.wait_ge(h2T_hi, KC * t + k + 1)
                    dve.tensor_tensor(h2Tl[:, k], ps[:, bank], h2Th[:, k].bitcast(F32), ALU.subtract)\
                       .then_inc(h2T_lo, 1)

            def tile2(t, first, last):
                for f in range(FT):
                    dve.wait_ge(sg2_ok, FT * t + f + 1)
                    dve.tensor_tensor(u2[:, f % 2], ps[:, 5 + 2 * (f % 2)], sg2[:, f % 2], ALU.mult)\
                       .then_inc(u2_ok, 1)
                    dve.wait_ge(u2_hi, FT * t + f + 1)
                    dve.tensor_tensor(u2l[:, f % 2], u2[:, f % 2], u2h[:, f % 2].bitcast(F32), ALU.subtract)\
                       .then_inc(u2_lo, 1)
                    if first:
                        split_pieces(dve, *due2(f), False)
                    if last and f:
                        split_pieces(dve, ENDS[1] + f - 1, ENDS[1] + f, False)
                    if last and f == 5:
                        stats3(0)
                    if last and f == 6:
                        aggregate3()
                    if last and f == 7:
                        norm3(0, range(SUB))
                if not last:
                    h2T_rest(t + 1)
                else:
                    split_pieces(dve, ENDS[1] + FT - 1, ENDS[2] - 1, False)
                    h2T_rest(TILES)
                    split_pieces(dve, ENDS[2] - 1, ENDS[2], False)
                dve.wait_ge(down2, FT * t + FT)
                dve.wait_ge(res_ok, t + 1)
                for s in range(SUB):
                    dve.tensor_tensor(res[:, s], res[:, s], ps[:, s], ALU.add).then_inc(y_ok, 1)

            h2T_rest(0)
            dve.wait_ge(x2_out, 16 * (STEPS - 1))
            add_residual(STEPS - 1, STEPS)
            split_pieces(dve, NP1 + 2, NP1 + 4, False)
            dve.wait_ge(x2_out, 16 * STEPS)
            tile2(0, True, False)
            with dve.Fori(1, TILES - 1) as t:
                tile2(t, False, False)
            tile2(TILES - 1, False, True)

            def xnT_rest(t):
                for k in range(KC):
                    if k == 0:
                        dve.wait_ge(xT_out, 32 * t)
                    dve.wait_ge(h2T_hi, KC * (t + TILES) + k + 1)
                    dve.tensor_tensor(h2Tl[:, k], ps[:, 4 + k], h2Th[:, k].bitcast(F32), ALU.subtract)\
                       .then_inc(h2T_lo, 1)

            def xT_copy(t):
                dve.wait_ge(xT_out, 32 * TILES)
                dve.wait_ge(xT_in, 32 * (t - TILES + 1))
                for k in range(KC):
                    dve.wait_ge(h2T_hi, KC * (t + TILES) + k + 1)
                    dve.tensor_copy(h2Tl[:, k], h2[:, k]).then_inc(h2T_lo, 1)

            def compare(n, m):
                if m == 0:
                    return
                first = m * (m - 1) // 2
                dve.wait_ge(ab_ok, 4 * n + m + 1)
                dve.tensor_tensor(cmp[:, first:first + m], ab[:, 0:m], ab[:, m:m + 1].broadcast_to([P, m, TOK]),
                                  ALU.is_ge).then_inc(cmp_ok, 1)
                if m == 2:
                    dve.wait_ge(cmp_ok, 3 * n + 2)
                    dve.tensor_tensor(win[:, 0], cmp[:, 0], cmp[:, 1], ALU.add).then_inc(win_ok, 1)
                    dve.tensor_tensor(win[:, 1], cmp[:, 2], cmp[:, 0], ALU.subtract).then_inc(win_ok, 1)
                    dve.tensor_tensor(win[:, 2], cmp[:, 1], cmp[:, 2], ALU.add).then_inc(win_ok, 1)

            def zero_losers(n):
                dve.wait_ge(cmp_ok, 3 * n + 3)
                dve.tensor_tensor(win[:, 3], cmp[:, 3], cmp[:, 4], ALU.add).then_inc(win_ok, 1)
                dve.wait_ge(win_ok, 4 * n + 3)
                dve.tensor_tensor(win[:, 0:2], win[:, 0:2], cmp[:, 3:5], ALU.add).then_inc(win2_ok, 1)
                dve.wait_ge(win_ok, 4 * n + 4)
                dve.tensor_tensor(win[:, 3], win[:, 3], cmp[:, 5], ALU.add).then_inc(win2_ok, 1)
                dve.tensor_tensor(win[:, 2], win[:, 2], cmp[:, 5], ALU.subtract).then_inc(win2_ok, 1)
                for m, op, bound, made in ((0, ALU.is_ge, 2.0, 1), (1, ALU.is_ge, 1.0, 1), (3, ALU.is_le, 1.0, 2),
                                           (2, ALU.is_le, 0.0, 3)):
                    dve.wait_ge(win2_ok, 3 * n + made)
                    dve.scalar_tensor_tensor(out=hh[:, m], in0=win[:, m], scalar=bound, in1=hh[:, m], op0=op,
                                             op1=ALU.mult).then_inc(kept, 1)

            def add_down(t, made):
                dve.wait_ge(down3, made)
                dve.wait_ge(acc_in, t)
                for s in range(SUB):
                    dve.tensor_tensor(res[:, s], res[:, s], ps[:, s], ALU.add).then_inc(acc_ok, 1)

            def tile3(t, first=False, norm=False, fetch=False, fresh=(), last=False):
                for s in range(SETS):
                    n = SETS * t + s
                    need(dve, u3_lo, 4 * n)
                    for m in range(4):
                        dve.wait_ge(sg3_ok, 4 * n + m + 1)
                        dve.tensor_tensor(hh[:, m], ps[:, 5 + 2 * (m % 2)], sg2[:, m % 2], ALU.mult)\
                           .then_inc(hh_ok, 1)
                        compare(n, m)
                        if fresh and fresh[4 * s + m] is not None:
                            split_pieces(dve, fresh[4 * s + m], fresh[4 * s + m] + 1, False)
                        if s == 0 and m == 0 and norm:
                            stats3(t + 1)
                        if s == 1 and m == 0 and norm:
                            aggregate3()
                        if s == 1 and m == 0 and not first:
                            add_down(16 * t, SETS * t)
                        if s == 1 and m in (1, 2) and norm:
                            norm3(t + 1, (2 * m - 2, 2 * m - 1))
                    if s == 1 and norm:
                        xnT_rest(t + 1)
                    if s == 1 and fetch:
                        xT_copy(t + 1)
                    zero_losers(n)
                    hi, lo = (h2Th, h2Tl) if last and s == 1 else (u3h, u3l)
                    for i, m in enumerate(MEMBERS):
                        dve.wait_ge(u3_hi, 4 * n + i + 1)
                        dve.tensor_tensor(lo[:, m], hh[:, m], hi[:, m].bitcast(F32), ALU.subtract)\
                           .then_inc(u3_lo, 1)

            for step3 in SCHEDULE3:
                run3(dve, tile3, *step3)
            dve.wait_ge(acc_in, 16 * HALVES * TILES)
            for s in range(SUB):
                dve.wait_ge(down3, SETS * HALVES * TILES + s)
                dve.tensor_tensor(res[:, s], res[:, s], ps[:, s], ALU.add).then_inc(acc_ok, 1)

        @block.tensor
        def _(pe):
            def hT_turn(t):
                pe.wait_ge(h_ok, t + 1)
                for k in range(KC):
                    ins = pe.transpose(ps[:, 7, k * P:k * P + P], h[:, k * P:k * P + P], ident)
                ins.then_inc(hT_ps, 1)

            def project(bank, piece, wide, col, weights=False):
                for k in range(KC):
                    at = piece + (k // 2 if wide == 512 else k)
                    lo = (k % 2) * 512 if wide == 512 else col
                    if weights:
                        pe.wait_ge(w_lo, at + 1)
                    ins = mm3(pe, ps[:, bank], hTh[:, k], hTl[:, k], *place(1, at, lo, 512), k == 0, k == KC - 1)
                return ins

            def onT_turn():
                for j in range(H):
                    ins = pe.transpose(ps[:, 4 + j // 4, (j % 4) * P:(j % 4) * P + P], sc[:, j], ident)
                    if j % 4 == 3:
                        ins.then_inc(onT_ps, 1)

            def out_project(heads=range(H)):
                for j in heads:
                    at, lo = O0 + j // 2, (j % 2) * 512
                    ins = mm3(pe, ps[:, 6], onTh[:, j], onTl[:, j], *place(1, at, lo, 512), j == 0, j == H - 1)
                if j == H - 1:
                    ins.then_inc(attn_ps, 1)

            def step(t, first=False, last=False, cross=True, update=True):
                pe.wait_ge(hT_lo, t + 1)
                project(0, Q0, 512, 0, first)
                project(1, K0, 512, 0, first).then_inc(qk_ps, 1)
                if not first:
                    pe.wait_ge(on_ok, t)
                    onT_turn()
                for j in range(2):
                    ins = project(2 + j, V0, 1024, 512 * j, first)
                ins.then_inc(v_ps, 1)
                if not first:
                    pe.wait_ge(onT_lo, 2 * t)
                    if update:
                        pe.wait_ge(state_sum, t)
                    else:
                        pe.wait_ge(state_sum, STEPS - B)
                        pe.wait_ge(x2_ok, t - 1)
                    if not cross:
                        pe.wait_ge(w_lo, NP1)
                    out_project()
                pe.wait_ge(qk_ok, t + 1)
                qkv = qk[:].rearrange("p h d -> p (h d)")
                for j in range(2 * PAIRS):
                    ins = pe.transpose(ps[:, j // PAIRS, (j % PAIRS) * P:(j % PAIRS) * P + P],
                                       qkv[:, j * P:j * P + P], ident)
                    if j % PAIRS == PAIRS - 1:
                        ins.then_inc(qkT_ps, 1)
                project(4, G0, 1024, 0, first).then_inc(g_ps, 1)
                pe.wait_ge(kT_ok, t + 1)
                pe.wait_ge(qT_ok, 2 * t + 2)
                for r in range(PAIRS):
                    ins = pe.matmul(ps[:, r // 2, (r % 2) * 256:(r % 2) * 256 + 256], kT[:, r],
                                    qbd[:, r].rearrange("p a i -> p (a i)"), start=True, stop=True)
                ins.then_inc(s_ps, 1)
                project(5, G0, 1024, 512, first).then_inc(g_ps, 1)
                if not last:
                    hT_turn(t + 1)
                pe.wait_ge(s_ok, t + 1)
                pe.wait_ge(v_ok, t + 1)
                if cross:
                    pe.wait_ge(state_ok, t + 1 if update else STEPS - B + 1)
                b = t % B
                for j in range(H):
                    o = ps[:, 2 + j // 4, (j % 4) * DV:(j % 4) * DV + DV]
                    if isinstance(t, int):
                        s_in = state[:, b, (j // 2) * DV:(j // 2) * DV + DV]
                    else:
                        s_in = state[:, bass.ds(b, 1), (j // 2) * DV:(j // 2) * DV + DV].rearrange("p a n -> p (a n)")
                    ins = pe.matmul(o, sc[:, j], v[:, j], start=True, stop=not cross)
                    if cross:
                        ins = pe.matmul(o, qbd[:, j // 2, j % 2], s_in, start=False, stop=True)
                ins.then_inc(o_ps, 1)
                if not update:
                    return
                if not first:
                    pe.wait_ge(x2_ok, t)
                for j in range(H):
                    ins = pe.matmul(ps[64 * (j % 2):64 * (j % 2) + 64, 6, (j // 2) * DV:(j // 2) * DV + DV],
                                    qk[:, H + j], v[:, j], start=True, stop=True)
                ins.then_inc(u_ps, 1)

            pe.wait_ge(consts_in, 32)
            hT_turn(0)
            step(0, first=True, cross=False)
            with pe.Fori(1, B) as t:
                step(t, cross=False)
            with pe.Fori(B, STEPS - B) as t:
                step(t)
            with pe.Fori(STEPS - B, STEPS - 1) as t:
                step(t, update=False)
            step(STEPS - 1, last=True, update=False)
            pe.wait_ge(on_ok, STEPS)
            onT_turn()
            pe.wait_ge(onT_lo, 2 * STEPS - 1)
            pe.wait_ge(x2_ok, STEPS - 1)
            out_project(range(0, 4))
            pe.wait_ge(onT_lo, 2 * STEPS)
            out_project(range(4, H - 2))

            def h2T_turn(k, bank):
                for s in range(SUB):
                    ins = pe.transpose(ps[:, bank, s * P:s * P + P], h2[:, s, k * P:k * P + P], ident)
                ins.then_inc(h2T_ps, 1)

            def up2(t, f, weights):
                if weights:
                    pe.wait_ge(w_lo, NP1 + f + f // 2 + 1)
                if f >= 2:
                    pe.wait_ge(u2_ok, FT * t + f - 1)
                if weights and f == 1:
                    pe.wait_ge(x2_ok, STEPS)
                for g in range(2):
                    for k in range(KC):
                        lo = 512 * g + P * k
                        ins = mm3(pe, ps[:, 4 + 2 * (f % 2) + g], *place(2, f, lo, P), h2Th[:, k], h2Tl[:, k],
                                  k == 0, k == KC - 1)
                ins.then_inc(up2_ps, 1)

            def down2_add(t, f, weights):
                if weights:
                    pe.wait_ge(w_lo, min(NP1 + 3 * (f // 2) + 3, ENDS[1]))
                pe.wait_ge(u2_lo, FT * t + f + 1)
                if f == 0 and (not isinstance(t, int) or t > 0):
                    pe.wait_ge(y_ok, SUB * t)
                for s in range(SUB):
                    ins = mm3(pe, ps[:, s], u2h[:, f % 2, s * P:s * P + P], u2l[:, f % 2, s * P:s * P + P],
                              *place(2, FT + f // 2, 512 * (f % 2), 512), f == 0, f == FT - 1)
                ins.then_inc(down2, 1)

            def tile2(t, first, last):
                pe.wait_ge(h2T_lo, KC * t + KC)
                for f in range(FT):
                    up2(t, f, first)
                    if f == FT - 1:
                        if last:
                            pe.wait_ge(xn_ok, SUB)
                        else:
                            pe.wait_ge(h2_ok, SUB * t + 2 * SUB)
                        pe.wait_ge(u2_ok, FT * t + FT - 1)
                        h2T_turn(0, 6)
                        h2T_turn(1, 7)
                    if f:
                        down2_add(t, f - 1, first)
                pe.wait_ge(u2_ok, FT * t + FT)
                h2T_turn(2, 4)
                h2T_turn(3, 5)
                down2_add(t, FT - 1, first)

            pe.wait_ge(h2_ok, SUB)
            for k, bank in enumerate(h2T_banks(0)):
                h2T_turn(k, bank)
            out_project(range(H - 2, H))
            tile2(0, True, False)
            with pe.Fori(1, TILES - 1) as t:
                tile2(t, False, False)
            tile2(TILES - 1, False, True)

            def up3(t, s, m, weights):
                n = 4 * (SETS * t + s) + m
                if s or m >= 2:
                    pe.wait_ge(hh_ok, n - 1)
                for g in range(2):
                    for k in range(KC):
                        at, lo = 4 * s + 2 * g + k // 2, 512 * (k % 2) + P * m
                        if weights and m == 0:
                            pe.wait_ge(w_lo, weights + at + 1)
                        ins = mm3(pe, ps[:, 4 + 2 * (m % 2) + g], *place(3, at, lo, P), h2Th[:, k], h2Tl[:, k],
                                  k == 0, k == KC - 1)
                ins.then_inc(up3_ps, 1)

            def down3_add(t, s, at, done):
                for i in at:
                    m = MEMBERS[i]
                    pe.wait_ge(u3_lo, 4 * (SETS * t + s) + i + 1)
                    for j in range(SUB):
                        ins = mm3(pe, ps[:, j], u3h[:, m, j * P:j * P + P], u3l[:, m, j * P:j * P + P],
                                  *place(3, 4 * SETS + 2 * s + m // 2, 512 * (m % 2), 512),
                                  s == 0 and i == 0, s == SETS - 1 and i == 3)
                if done:
                    ins.then_inc(down3, 1)

            def tile3(t, first=False, norm=False, fetch=False, fresh=(), last=False):
                weights = ENDS[1] if first else ENDS[2] if isinstance(t, int) and t == TILES else 0
                pe.wait_ge(h2T_lo, KC * (t + TILES) + KC)
                for m in range(4):
                    up3(t, 0, m, weights)
                if not first:
                    down3_add(t - 1, 1, range(4), True)
                for m in range(4):
                    up3(t, 1, m, weights)
                if weights:
                    pe.wait_ge(w_lo, weights + 4 * SETS + 2)
                if norm:
                    pe.wait_ge(xn_ok, SUB * t + 2 * SUB)
                    pe.wait_ge(hh_ok, 4 * SETS * t + 4 * SETS - 1)
                    h2T_turn(0, 4)
                    h2T_turn(1, 5)
                if first:
                    pe.wait_ge(y_ok, SUB * TILES)
                else:
                    pe.wait_ge(acc_ok, SUB * t)
                down3_add(t, 0, range(0, 2), False)
                if norm:
                    pe.wait_ge(hh_ok, 4 * SETS * t + 4 * SETS)
                    h2T_turn(2, 6)
                    h2T_turn(3, 7)
                down3_add(t, 0, range(2, 4), True)
                if weights:
                    pe.wait_ge(w_lo, weights + NP3)

            for step3 in SCHEDULE3:
                run3(pe, tile3, *step3)
            pe.wait_ge(u3_lo, 4 * SETS * HALVES * TILES)
            for j in range(SUB):
                for m in range(4):
                    ins = mm3(pe, ps[:, j], h2Th[:, m, j * P:j * P + P], h2Tl[:, m, j * P:j * P + P],
                              *place(3, 4 * SETS + 2 + m // 2, 512 * (m % 2), 512), False, m == 3)
                ins.then_inc(down3, 1)


_INS = ["hidden_states", "attn_norm_w", "q_w", "k_w", "v_w", "g_w", "o_w", "gnorm_w", "mlp_norm_w",
        "gate_w", "down_w"]
_FFN = ["w_gate", "w_up", "w_down"]


def _constants():
    import numpy as np

    f = np.float32
    inv = (f(1.0) / np.power(f(10000.0), np.arange(0, DK, 2, dtype=f) / f(DK))).astype(f)
    ang = (np.arange(L, dtype=f)[:, None] * inv).astype(f).astype(np.float64)
    cos, sin = np.cos(ang), np.sin(ang)
    by_chunk = lambda a: a.reshape(CH, P, DK).transpose(1, 0, 2).reshape(P, CH * DK)
    gamma = 1.0 - 2.0 ** (-5.0 - np.arange(H))
    i = np.arange(P)
    t = np.zeros((P, NCONST), np.float32)
    t[:, COS:COS + CH * DK] = by_chunk(np.concatenate([cos, cos], 1))
    t[:, SIN:SIN + CH * DK] = by_chunk(np.concatenate([-sin, sin], 1))
    t[:, DEC:DEC + H] = gamma[None] ** (i[:, None] + 1.0) * DK ** -0.5
    t[:, DEC + H:DEC + 2 * H] = gamma[None] ** -(i[:, None] + 1.0)
    for r in range(PAIRS):
        for a in range(2):
            t[64 * a:64 * a + 64, GAM + r * DV:GAM + (r + 1) * DV] = gamma[2 * r + a] ** P
    t[:, MASK:MASK + P] = i[:, None] <= i[None, :]
    t[:, IDN:IDN + P] = np.eye(P)
    return t


def kernel(**inputs):
    import numpy as _np
    import concourse.bacc as _bacc
    from concourse import mybir as _mybir
    from concourse.bass_utils import run_bass_kernel_spmd as _run

    nc = _bacc.Bacc("TRN2", target_bir_lowering=False, num_devices=1)
    arrays, args = {}, []
    named = [("L0_attn_" + n) for n in _INS] + [("L0_ffn_" + n) for n in _FFN]
    for name in named:
        arrays[name] = _np.ascontiguousarray(inputs[name])
    arrays["constants"] = _constants()
    for name, a in arrays.items():
        args.append(nc.dram_tensor(name, a.shape, _mybir.dt.from_np(a.dtype), kind="ExternalInput").ap())
    out = nc.dram_tensor("out_0", (B, L, D), _mybir.dt.float32, kind="ExternalOutput").ap()
    build_program(nc, *args, out)
    r = _run(nc, [arrays], core_ids=[0])
    return r.results[0]["out_0"]
```
